# Optimizing a Trainium2 kernel written in Bass

```python
import numpy as np
import jax
import jax.numpy as jnp

def _softmax(x, axis=-1):
    return jax.nn.softmax(x, axis=axis)

def _gelu(x):
    return jax.nn.gelu(x, approximate=True)

def _silu(x):
    return jax.nn.silu(x)

def _sigmoid(x):
    return jax.nn.sigmoid(x)

def _layernorm(x, axis=-1, eps=1e-05):
    m = jnp.mean(x, axis=axis, keepdims=True)
    v = jnp.var(x, axis=axis, keepdims=True)
    return (x - m) / jnp.sqrt(v + eps)

def _scatter_add(tgt, idx, src, axis=0):
    return tgt.at[idx].add(src)

def _segment_sum(src, seg, n):
    return jax.ops.segment_sum(src, seg, n)
kernel_name = 'mk_pixart_seq_d1_seqx_r2_deb1ea'

def setup_inputs(seed: int=0):
    np.random.seed(seed)
    _w = jnp.asarray

    def _rec_inputs():
        import jax
        import jax.numpy as jnp
        _rk = jax.random.key(seed)
        x = -0.0003929 + 0.9999 * jax.random.normal(jax.random.fold_in(_rk, 1), (16, 512, 512), jnp.float32)
        _lenS = 512 - jax.random.randint(jax.random.fold_in(_rk, 7), (16,), 0, max(1, 512 // 4) + 1, jnp.int32)
        _lenS2 = 120 - jax.random.randint(jax.random.fold_in(_rk, 8), (16,), 0, max(1, 120 // 4) + 1, jnp.int32)
        _ctx_1024P = jax.random.normal(jax.random.fold_in(_rk, 11), (16, 16, 512), jnp.float32)
        _ctx_1024c = jax.random.dirichlet(jax.random.fold_in(_rk, 511), 0.3 * jnp.ones((16,), jnp.float32), (16, 120))
        _ctx_1024t = jnp.einsum('bsk,bkd->bsd', _ctx_1024c, _ctx_1024P)
        _ctx_1024t = _ctx_1024t * jax.lax.rsqrt(jnp.mean(jnp.square(_ctx_1024t)) + 1e-12) * 0.953939
        ctx_1024 = -1.39393e-06 + 0.999914 * (_ctx_1024t + 0.3 * jax.random.normal(jax.random.fold_in(_rk, 611), (16, 120, 512), jnp.float32))
        cond_1024 = -0.00920427 + 1.00102 * jax.random.normal(jax.random.fold_in(_rk, 12), (16, 512), jnp.float32)
        return (x, ctx_1024, cond_1024)
    x, ctx_1024, cond_1024 = _rec_inputs()

    def _L0_xcond_setup():
        import jax, jax.numpy as jnp
        import numpy as np
        EPS = 1e-05

        def _ada_ln(x, c, W_ss, b_ss):
            mu = jnp.mean(x, axis=-1, keepdims=True)
            var = jnp.mean((x - mu) ** 2, axis=-1, keepdims=True)
            h = (x - mu) / jnp.sqrt(var + EPS)
            ss = jax.nn.silu(c) @ W_ss + b_ss
            scale, bias = jnp.split(ss, 2, axis=-1)
            return (1.0 + scale)[:, None, :] * h + bias[:, None, :]
        key = jax.random.key(seed)
        ks = jax.random.split(key, 12)
        B, Lq, Lkv, H = (8, 1024, 256, 512)
        s = 0.02
        return {'x_q': jax.random.normal(ks[0], (B, Lq, H), jnp.float32), 'x_kv': jax.random.normal(ks[1], (B, Lkv, H), jnp.float32), 't_vec': jax.random.normal(ks[2], (B, H), jnp.float32), 'Wq': jax.random.normal(ks[3], (H, H), jnp.float32) * s, 'bq': jnp.zeros((H,), jnp.float32), 'Wkv': jax.random.normal(ks[4], (H, 2 * H), jnp.float32) * s, 'bkv': jnp.zeros((2 * H,), jnp.float32), 'Wp': jax.random.normal(ks[5], (H, H), jnp.float32) * s, 'bp': jnp.zeros((H,), jnp.float32), 'Wss_q': jax.random.normal(ks[6], (H, 2 * H), jnp.float32) * s, 'bss_q': jnp.zeros((2 * H,), jnp.float32), 'Wss_kv': jax.random.normal(ks[7], (H, 2 * H), jnp.float32) * s, 'bss_kv': jnp.zeros((2 * H,), jnp.float32)}
    _L0_xcond_all = _L0_xcond_setup()
    _L0_xcond_in = {k: v for k, v in _L0_xcond_all.items() if k in ('Wq', 'bq', 'Wkv', 'bkv', 'Wp', 'bp', 'Wss_q', 'bss_q', 'Wss_kv', 'bss_kv')}
    del _L0_xcond_all
    return {'x': x, 'ctx_1024': ctx_1024, 'cond_1024': cond_1024, 'L0_xcond_Wq': _L0_xcond_in['Wq'], 'L0_xcond_bq': _L0_xcond_in['bq'], 'L0_xcond_Wkv': _L0_xcond_in['Wkv'], 'L0_xcond_bkv': _L0_xcond_in['bkv'], 'L0_xcond_Wp': _L0_xcond_in['Wp'], 'L0_xcond_bp': _L0_xcond_in['bp'], 'L0_xcond_Wss_q': _L0_xcond_in['Wss_q'], 'L0_xcond_bss_q': _L0_xcond_in['bss_q'], 'L0_xcond_Wss_kv': _L0_xcond_in['Wss_kv'], 'L0_xcond_bss_kv': _L0_xcond_in['bss_kv']}

def reference(x, ctx_1024, cond_1024, L0_xcond_Wq, L0_xcond_bq, L0_xcond_Wkv, L0_xcond_bkv, L0_xcond_Wp, L0_xcond_bp, L0_xcond_Wss_q, L0_xcond_bss_q, L0_xcond_Wss_kv, L0_xcond_bss_kv):
    import jax
    import jax.numpy as jnp

    def _L0_xcond_ref(x_q, x_kv, t_vec, Wq, bq, Wkv, bkv, Wp, bp, Wss_q, bss_q, Wss_kv, bss_kv):
        import jax, jax.numpy as jnp
        import numpy as np
        EPS = 1e-05

        def _ada_ln(x, c, W_ss, b_ss):
            mu = jnp.mean(x, axis=-1, keepdims=True)
            var = jnp.mean((x - mu) ** 2, axis=-1, keepdims=True)
            h = (x - mu) / jnp.sqrt(var + EPS)
            ss = jax.nn.silu(c) @ W_ss + b_ss
            scale, bias = jnp.split(ss, 2, axis=-1)
            return (1.0 + scale)[:, None, :] * h + bias[:, None, :]
        B, Lq, H = x_q.shape
        Lkv = x_kv.shape[1]
        nh = 16
        dh = H // nh
        xq = _ada_ln(x_q, t_vec, Wss_q, bss_q)
        xkv = _ada_ln(x_kv, t_vec, Wss_kv, bss_kv)
        q = (xq @ Wq + bq).reshape(B, Lq, nh, dh)
        kv = (xkv @ Wkv + bkv).reshape(B, Lkv, 2, nh, dh)
        k = kv[:, :, 0]
        v = kv[:, :, 1]
        scores = jnp.einsum('bqhd,bkhd->bhqk', q, k) / jnp.sqrt(jnp.float32(dh))
        attn = jax.nn.softmax(scores, axis=-1)
        out = jnp.einsum('bhqk,bkhd->bqhd', attn, v).reshape(B, Lq, H)
        return x_q + (out @ Wp + bp)
    x = _L0_xcond_ref(x, ctx_1024, cond_1024, L0_xcond_Wq, L0_xcond_bq, L0_xcond_Wkv, L0_xcond_bkv, L0_xcond_Wp, L0_xcond_bp, L0_xcond_Wss_q, L0_xcond_bss_q, L0_xcond_Wss_kv, L0_xcond_bss_kv)
    return x

_drawn_inputs = setup_inputs


def setup_inputs(seed=0):
    import zlib

    import numpy as np

    out = dict(_drawn_inputs(seed))
    spreads = {'L0_xcond_bq': (0.0, 2.0),
     'L0_xcond_bkv': (0.0, 0.1),
     'L0_xcond_bp': (0.0, 0.1),
     'L0_xcond_bss_q': (0.0, 0.8),
     'L0_xcond_bss_kv': (0.0, 0.341)}
    factors = {'L0_xcond_Wq': 6.512, 'L0_xcond_Wss_q': 8.0}
    for name, (base, spread) in spreads.items():
        noise = np.random.default_rng([zlib.crc32(name.encode()), seed]).standard_normal(out[name].shape)
        drawn = base * np.exp(spread * noise) if base else spread * noise
        out[name] = jnp.asarray(drawn.astype(out[name].dtype))
    for name, factor in factors.items():
        out[name] = (out[name] * factor).astype(out[name].dtype)
    return out
```

```python
import concourse.bass as bass
from concourse import mybir
from contextlib import ExitStack


def adaln_cross_attention_kernel(
    nc: bass.Bass,
    x: bass.AP,
    ctx_kv: bass.AP,
    cond: bass.AP,
    Wq: bass.AP,
    bq: bass.AP,
    Wkv: bass.AP,
    bkv: bass.AP,
    Wp: bass.AP,
    bp: bass.AP,
    Wss_q: bass.AP,
    bss_q: bass.AP,
    Wss_kv: bass.AP,
    bss_kv: bass.AP,
    out: bass.AP,
):
    f32, f32r = mybir.dt.float32, mybir.dt.float32r
    ALU, ACT, AX = mybir.AluOpType, mybir.ActivationFunctionType, mybir.AxisListType

    P = 128
    NB, L, D = x.shape
    KV = ctx_kv.shape[1]
    NH = 16
    DH = D // NH
    NC = D // P
    NT = L // P
    HG = P // DH
    EPS = 1e-5
    SCALE = float(DH) ** -0.5
    UNITS = NB * NC
    PAIR = 2 * NC
    GB = 4
    NG = NB // GB
    GN = GB * KV
    KS = 3 * DH + 2
    XT_AHEAD, OUT_BEHIND = 5, 5
    HI, LO = 0, 1
    PASSES = ((HI, HI), (HI, LO), (LO, HI))
    assert NC == NT == HG == 4 and 3 * DH == 96

    x_tiles = x.rearrange("b (t p) n -> (b t) p n", p=P)
    out_tiles = out.rearrange("b (t p) n -> (b t) p n", p=P)
    k_scratch = nc.dram_tensor("k_scratch", [2, NC, P, NB * KV], f32, kind="Internal").ap()
    v_scratch = nc.dram_tensor("v_scratch", [NB, KV, D], f32, kind="Internal").ap()

    ctx = ExitStack()
    with ctx:
        def sb(name, shape, dt=f32, where=ctx):
            return where.enter_context(nc.sbuf_tensor(name, shape, dt))

        def sem(name):
            return ctx.enter_context(nc.semaphore(name))

        with ExitStack() as early:
            wss = [sb("wss_kv", [P, NC, 2 * D], f32, early), sb("wss_q", [P, NC, 2 * D], f32, early)]
        xT = sb("xT", [P, 2, 2, NC, L], f32r)
        wq = sb("wq", [P, 2, NC, D], f32r)
        wp = sb("wp", [P, 2, NC, D], f32r)
        outT = sb("outT", [P, 2, 2 * NC, L], f32r)
        stack = sb("stack", [P, 2, HG, L], f32r)
        qT = sb("qT", [P, 2, 2, L], f32r)
        xin = sb("xin", [P, 2, NT, D])
        xres = sb("xres", [P, 4, D])
        h = sb("h", [P, NT, D])
        probs = sb("probs", [P, 2, HG, L])
        onorm = sb("onorm", [P, 2, L])
        rsum = sb("rsum", [P, L])
        xaff = sb("xaff", [P, 2, L])
        kst = sb("kst", [P, 2, HG, KV], f32r)
        kh = sb("kh", [P, 2, KV], f32r)
        kbd = sb("kbd", [P, 2, HG, KV], f32r)
        vt = sb("vt", [P, 2, D])
        bp_bc = sb("bp_bc", [P, D])
        bv_bc = sb("bv_bc", [P, D])
        ident = sb("ident", [P, P])
        ones = sb("ones", [P, DH])
        headmask = sb("headmask", [P, HG])
        minus_half = sb("minus_half", [P, 4])
        eps4 = sb("eps4", [P, 4])
        vecrows = sb("vecrows", [24, P])
        vecs = sb("vecs", [P, 24])
        crow = sb("crow", [NB, D])
        cexp = sb("cexp", [NB, D])
        csilu = sb("csilu", [NB, D])
        csT = sb("csT", [P, NC, NB])
        aff = [sb("aff_kv", [P, 2 * NC, NB]), sb("aff_q", [P, 2 * NC, NB])]
        one_zero = sb("one_zero", [P, 2 * NC])
        affb = sb("affb", [P, 2, 2 * NC])
        bst = sb("bst", [P, 4, 6])
        mv = sb("mv", [P, 2, 4, 2])
        rstd = sb("rstd", [P, 2, 4])
        mneg = sb("mneg", [P, NT, HG])
        mhl = sb("mhl", [P, NT, 2 * HG], f32r)
        mT = sb("mT", [2 * HG, 2, L], f32r)

        def wk(hl, k):
            return outT[:, hl, k, :]

        def wv(hl, k):
            return outT[:, hl, NC + k, :]

        def ctxT(hl, k):
            return stack[:, hl, k, 0:GN]

        hctx, cin = probs[0:KV, 0], probs[0:KV, 1]

        def f(ap):
            return ap.bitcast(f32)

        S = ctx.enter_context(nc.psum_tensor("S", [P, 4, 512], f32))
        pA = ctx.enter_context(nc.psum_tensor("pA", [P, 512], f32))
        pB = ctx.enter_context(nc.psum_tensor("pB", [P, 512], f32))
        pV = ctx.enter_context(nc.psum_tensor("pV", [P, 512], f32))
        pD = ctx.enter_context(nc.psum_tensor("pD", [P, 512], f32))
        KVB = (pA, pB, pV, pD)

        s_wss = [sem("s_wss_kv_in"), sem("s_wss_q_in")]
        s_cond, s_vecrows, s_bcast = sem("s_cond_in"), sem("s_vecrows_in"), sem("s_bcast_in")
        s_win = [sem(f"s_weight_in{n}") for n in range(4)]
        s_ctx = sem("s_ctx_in")
        s_const, s_ident, s_mask = sem("s_const"), sem("s_ident"), sem("s_mask")
        s_cexp, s_cden, s_crec, s_silu = sem("s_cexp"), sem("s_cden"), sem("s_crec"), sem("s_silu")
        s_early, s_earlyc = sem("s_early_transposed"), sem("s_early_copied")
        s_ss, s_ssb, s_aff = sem("s_ss"), sem("s_ss_biased"), sem("s_aff")
        s_whi, s_wlo = sem("s_weight_hi"), sem("s_weight_lo")
        s_cst, s_cag, s_cve, s_crs = sem("s_ctx_stats"), sem("s_ctx_aggr"), sem("s_ctx_vareps"), sem("s_ctx_rstd")
        s_hctx = sem("s_ctx_normalised")
        s_ct, s_ctm, s_ctb, s_cthi, s_ctlo = (sem("s_ctxT"), sem("s_ctxT_scaled"), sem("s_ctxT_biased"),
                                              sem("s_ctxT_hi"), sem("s_ctxT_lo"))
        s_kv, s_kvout, s_khi = sem("s_kv_product"), sem("s_kv_evacuated"), sem("s_k_hi")
        s_kst_out = [sem("s_k_stored0"), sem("s_k_stored1")]
        s_v_out = [sem("s_v_stored0"), sem("s_v_stored1")]
        s_x = [sem("s_x_in0"), sem("s_x_in1")]
        s_xres = [sem(f"s_xres_in{n}") for n in range(4)]
        s_store = [sem(f"s_y_stored{n}") for n in range(4)]
        s_kst = [sem("s_kst_in0"), sem("s_kst_in1")]
        s_kh = [sem("s_kh_in0"), sem("s_kh_in1")]
        s_v = [sem("s_v_in0"), sem("s_v_in1")]
        s_qst = [sem("s_qstack_in0"), sem("s_qstack_in1")]
        s_mst = [sem("s_mstack_in0"), sem("s_mstack_in1")]
        (u_qproj, u_qhi, u_qlo, u_kbd, u_smax, u_mneg, u_mhi, u_msplit, u_mt, u_mtc, u_st, u_exp, u_av, u_rsum,
         u_onorm, u_ohi, u_olo, u_out, u_resb, u_y, u_xt, u_xaff, u_xlo) = (sem("u_" + n) for n in (
            "qproj qhi qlo kbd smax mneg mhi msplit mt mtcopied st exp av rsum onorm outhi outlo out "
            "resbiased y xt xaff xlo").split())
        b_stats, b_aggr, b_vareps, b_rstd, b_h, b_aff = (sem("b_" + n) for n in
                                                         "stats aggr vareps rstd h aff".split())

        block = ctx.enter_context(nc.Block())

        def is_first(g):
            return isinstance(g, int) and g == 0

        class Step:

            def __init__(self, i, k):
                self.i, self.k = i, k
                self.static = isinstance(i, int)

            def has(self, d):
                return not self.static or 0 <= PAIR * self.i + self.k + d < UNITS

            def unit(self, d):
                return self.i * PAIR + (self.k + d)

            def batch(self, d):
                return self.i * 2 + (self.k + d) // NC

            def chunk(self, d):
                return (self.k + d) % NC

            def wait(self, eng, s, d, per=1, base=0):
                if not self.static:
                    eng.wait_ge(s, self.i * (PAIR * per) + ((self.k + d + 1) * per + base))
                    return
                n = min(PAIR * self.i + self.k + d + 1, UNITS)
                if n > 0:
                    eng.wait_ge(s, n * per + base)

            def wait_batch(self, eng, s, d, back=0):
                if not self.static:
                    eng.wait_ge(s, self.i * 2 + ((self.k + d) // NC + 1 - back))
                    return
                n = (PAIR * self.i + self.k + d) // NC + 1 - back
                if n > 0:
                    eng.wait_ge(s, n)

            def wait_units_of_batch(self, eng, s, d, back=0):
                if not self.static:
                    eng.wait_ge(s, self.i * PAIR + ((self.k + d) // NC + 1 - back) * NC)
                    return
                n = ((PAIR * self.i + self.k + d) // NC + 1 - back) * NC
                if n > 0:
                    eng.wait_ge(s, n)

            def wait_ring(self, eng, sems, d, dmas=1):
                m = len(sems)
                s = sems[(self.k + d) % m]
                if not self.static:
                    eng.wait_ge(s, self.i * (PAIR // m * 16 * dmas) + ((self.k + d) // m + 1) * 16 * dmas)
                    return
                n = (PAIR * self.i + self.k + d) // m + 1
                if n > 0:
                    eng.wait_ge(s, n * 16 * dmas)

            def wait_batch_dma(self, eng, sems, d):
                bk = (self.k + d) // NC
                if not self.static:
                    eng.wait_ge(sems[bk % 2], self.i * 16 + (bk // 2 + 1) * 16)
                    return
                eng.wait_ge(sems[bk % 2], ((2 * self.i + bk) // 2 + 1) * 16)

        def steps(eng, step):
            for k in range(-XT_AHEAD - 3, PAIR):
                step(Step(0, k))
            with eng.Fori(1, NB // 2 - 1) as i:
                for k in range(PAIR):
                    step(Step(i, k))
            for k in range(PAIR + OUT_BEHIND):
                step(Step(NB // 2 - 1, k))

        @block.sync
        def _(sp):
            sp.dma_start(crow[:, :], cond).then_inc(s_cond, 16)
            for row, src in ((0, bss_kv), (8, bss_q), (16, bq), (20, bkv[0:D])):
                n = src.shape[0] // P
                sp.dma_start(vecrows[row:row + n, :], src.rearrange("(a n) -> a n", n=P)).then_inc(s_vecrows, 16)
            sp.dma_start(wss[0][:, :, :], Wss_kv.rearrange("(k p) n -> p k n", p=P)).then_inc(s_wss[0], 16)
            sp.dma_start(cin, ctx_kv[0:GB].rearrange("b t n -> t b n")).then_inc(s_ctx, 16)
            weights = [Wkv[:, 0:D], Wkv[:, D:2 * D], Wq, Wp]
            for n in range(2):
                sp.dma_start(xin[:, n], weights[n].rearrange("(k p) n -> p k n", p=P)).then_inc(s_win[n], 16)
            sp.dma_start(wss[1][:, :, :], Wss_q.rearrange("(k p) n -> p k n", p=P)).then_inc(s_wss[1], 16)
            sp.dma_start(bp_bc[:, :], bp.rearrange("(a n) -> a n", a=1).broadcast_to([P, D])).then_inc(s_bcast, 16)
            sp.dma_start(bv_bc[:, :], bkv[D:2 * D].rearrange("(a n) -> a n", a=1).broadcast_to([P, D])).then_inc(s_bcast, 16)
            for n in range(2, 4):
                sp.wait_ge(s_whi, n - 1)
                sp.wait_ge(s_wlo, n - 1)
                sp.dma_start(xin[:, n - 2], weights[n].rearrange("(k p) n -> p k n", p=P)).then_inc(s_win[n], 16)

            def store_group(g):
                for c in range(NC):
                    sp.wait_ge(s_kvout, g * (NC + GB) + (c + 1))
                    for hl in (HI, LO):
                        sp.dma_start(k_scratch[hl, c, :, bass.ds(g * GN, GN)], f(qT[:, c % 2, hl, 0:GN]))\
                          .then_inc(s_kst_out[c % 2], 16)
                for b in range(GB):
                    sp.wait_ge(s_kvout, g * (NC + GB) + (NC + b + 1))
                    sp.dma_start(v_scratch[bass.ds(g * GB + b, 1)].rearrange("a t n -> (a t) n"), onorm[0:KV, b % 2, :])\
                      .then_inc(s_v_out[b % 2], 16)

            with sp.Fori(0, NG - 1) as g:
                sp.wait_ge(s_hctx, g + 1)
                sp.dma_start(cin, ctx_kv[bass.ds(g * GB + GB, GB)].rearrange("b t n -> t b n")).then_inc(s_ctx, 16)
                store_group(g)
            store_group(NG - 1)
            for par in range(2):
                sp.wait_ge(s_kst_out[par], 16 * 2 * NG * NC // 2)
                sp.wait_ge(s_v_out[par], 16 * NG * GB // 2)

            def step(t):
                d = XT_AHEAD + 3
                if t.chunk(d) == 0 and t.has(d):
                    if t.static and 2 * t.i + (t.k + d) // NC < 2:
                        sp.wait_ge(s_whi, 4)
                        sp.wait_ge(s_wlo, 4)
                    t.wait_batch(sp, b_h, d, back=2)
                    par = ((t.k + d) // NC) % 2
                    sp.dma_start(xin[:, par], x[bass.ds(t.batch(d), 1)].rearrange("a (t p) n -> p (a t) n", p=P))\
                      .then_inc(s_x[par], 16)
                if t.chunk(2) == 0 and t.has(2):
                    t.wait_units_of_batch(sp, u_av, 2, back=2)
                    par = ((t.k + 2) // NC) % 2
                    sp.dma_start(vt[0:KV, par, :], v_scratch[bass.ds(t.batch(2), 1)].rearrange("a t n -> (a t) n"))\
                      .then_inc(s_v[par], 16)
                if t.has(-3):
                    if not (t.static and t.i == 0 and t.k - 3 < 4):
                        t.wait_ring(sp, s_store, -7)
                    slot = (t.k - 3) % 4
                    sp.dma_start(xres[:, slot, :],
                                 x_tiles[bass.ds(t.unit(-3), 1)].rearrange("a p n -> (a p) n")).then_inc(s_xres[slot], 16)
                if t.has(2):
                    t.wait(sp, u_kbd, 0)
                    sp.dma_start(f(kh[:, t.k % 2, :]), k_scratch[HI, t.chunk(2), :, bass.ds(t.batch(2) * KV, KV)])\
                      .then_inc(s_kh[t.k % 2], 16)
                if t.has(1):
                    par = (t.k + 1) % 2
                    t.wait(sp, u_st, -1)
                    for s, hl in enumerate((HI, LO, HI)):
                        sp.dma_start(f(kst[DH * s:DH * (s + 1), par]),
                                     k_scratch[hl, t.chunk(1), :, bass.ds(t.batch(1) * KV, KV)]
                                     .rearrange("(j r) n -> r j n", r=DH)).then_inc(s_kst[par], 16)
                    t.wait(sp, u_qlo, 1)
                    for s, hl in enumerate((HI, HI, LO)):
                        for j in range(HG):
                            sp.dma_start(f(stack[DH * s:DH * (s + 1), par, j, :]),
                                         f(qT[DH * j:DH * (j + 1), par, hl, :])).then_inc(s_qst[par], 16)
                if t.has(0):
                    t.wait(sp, u_mtc, 0)
                    sp.dma_start(f(stack[3 * DH:KS, t.k % 2]), f(mT[:, t.k % 2, :]))\
                      .then_inc(s_mst[t.k % 2], 16)
                if t.has(-OUT_BEHIND):
                    t.wait(sp, u_y, -OUT_BEHIND)
                    slot = (t.k - OUT_BEHIND) % 4
                    sp.dma_start(out_tiles[bass.ds(t.unit(-OUT_BEHIND), 1)].rearrange("a p n -> (a p) n"),
                                 xres[:, slot, :]).then_inc(s_store[slot], 16)

            steps(sp, step)
            for s in s_store:
                sp.wait_ge(s, 16 * UNITS // 4)

        @block.gpsimd
        def _(pool):
            gp = nc.gpsimd
            gp.memset(ident[:, :], 0.0).then_inc(s_ident, 1)
            pool.wait_ge(s_ident, 1)
            gp.affine_select(out=ident[:, :], in_=ident[:, :], compare_op=ALU.not_equal, fill=1.0, base=0,
                             pattern=[[-1, P]], channel_multiplier=1).then_inc(s_ident, 1)
            pool.wait_ge(s_ident, 2)
            gp.memset(headmask[:, :], 1.0).then_inc(s_mask, 1)
            pool.wait_ge(s_mask, 1)
            gp.affine_select(out=headmask[:, :], in_=headmask[:, :], compare_op=ALU.is_ge, fill=0.0, base=0,
                             pattern=[[-DH, HG]], channel_multiplier=1).then_inc(s_mask, 1)
            pool.wait_ge(s_mask, 2)
            gp.affine_select(out=headmask[:, :], in_=headmask[:, :], compare_op=ALU.is_ge, fill=0.0, base=DH - 1,
                             pattern=[[DH, HG]], channel_multiplier=-1).then_inc(s_mask, 1)
            pool.wait_ge(s_mask, 3)
            pool.wait_ge(s_const, 1)
            pool.wait_ge(s_ssb, 1)
            gp.tensor_scalar(aff[0][:, 0:NC, :], aff[0][:, 0:NC, :], 1.0, None, ALU.add).then_inc(s_aff, 1)
            pool.wait_ge(s_aff, 1)
            with pool.Fori(0, NG) as g:
                pool.wait_ge(s_cag, g + 1)
                gp.tensor_tensor(rstd[0:KV, 0, :], mv[0:KV, 0, :, 1], eps4[0:KV, :], ALU.add).then_inc(s_cve, 1)
                pool.wait_ge(s_cve, g + 1)
                gp.tensor_tensor(rstd[0:KV, 0, :], rstd[0:KV, 0, :], minus_half[0:KV, :], ALU.pow).then_inc(s_crs, 1)
                for k in range(NC):
                    pool.wait_ge(s_ctm, g * NC + (k + 1))
                    t3 = xaff[:, k % 2, 0:GN].rearrange("p (b t) -> p b t", b=GB)
                    bias = aff[0][:, NC + k, bass.ds(g * GB, GB)].rearrange("p (b a) -> p b a", a=1)\
                        .broadcast_to([P, GB, KV])
                    gp.tensor_tensor(t3, t3, bias, ALU.add).then_inc(s_ctb, 1)
                    pool.wait_ge(s_cthi, g * NC + (k + 1))
                    gp.tensor_tensor(ctxT(LO, k), xaff[:, k % 2, 0:GN], f(ctxT(HI, k)), ALU.subtract)\
                      .then_inc(s_ctlo, 1)
            pool.wait_ge(s_bcast, 32)

            def step(t):
                w = XT_AHEAD - 1
                if t.has(XT_AHEAD + 1) and t.chunk(XT_AHEAD + 1) == 0:
                    par = ((t.k + XT_AHEAD + 1) // NC) % 2
                    t.wait_batch(pool, b_aggr, XT_AHEAD + 1)
                    gp.tensor_tensor(rstd[:, par, :], mv[:, par, :, 1], eps4[:, :], ALU.add).then_inc(b_vareps, 1)
                    t.wait_batch(pool, b_vareps, XT_AHEAD + 1)
                    gp.tensor_tensor(rstd[:, par, :], rstd[:, par, :], minus_half[:, :], ALU.pow).then_inc(b_rstd, 1)
                if t.has(w):
                    par, k = ((t.k + w) // NC) % 2, t.chunk(w)
                    t.wait(pool, u_xaff, w)
                    gp.tensor_tensor(xT[:, LO, par, k, :], xaff[:, (t.k + w) % 2, :], f(xT[:, HI, par, k, :]),
                                     ALU.subtract).then_inc(u_xlo, 1)
                if t.has(1):
                    par = (t.k + 1) % 2
                    t.wait_ring(pool, s_kh, 1)
                    t.wait(pool, u_smax, -1)
                    gp.tensor_tensor(kbd[:, par],
                                     f(kh[:, par, :]).rearrange("p (a n) -> p a n", a=1).broadcast_to([P, HG, KV]),
                                     headmask[:, :].rearrange("p (j a) -> p j a", a=1).broadcast_to([P, HG, KV]),
                                     ALU.mult).then_inc(u_kbd, 1)
                if t.has(-2):
                    t.wait(pool, u_ohi, -2)
                    gp.tensor_tensor(outT[:, LO, (t.k - 2) % (2 * NC), :], onorm[:, t.k % 2, :],
                                     f(outT[:, HI, (t.k - 2) % (2 * NC), :]), ALU.subtract).then_inc(u_olo, 1)
                if t.has(-4):
                    slot = t.k % 4
                    t.wait_ring(pool, s_xres, -4)
                    gp.tensor_tensor(xres[:, slot, :], xres[:, slot, :], bp_bc[:, :], ALU.add).then_inc(u_resb, 1)

            steps(pool, step)

        @block.scalar
        def _(act):
            sc = nc.scalar
            act.wait_ge(s_cond, 16)
            sc.activation(cexp[:, :], crow[:, :], ACT.Exp, scale=-1.0).then_inc(s_cexp, 1)
            weights = [outT[:, HI, 0:NC], outT[:, HI, NC:2 * NC], wq[:, HI], wp[:, HI]]
            for n, hi in enumerate(weights):
                act.wait_ge(s_win[n], 16)
                sc.activation(hi, xin[:, n % 2], ACT.Copy).then_inc(s_whi, 1)

            def group(g):
                for k in range(NC):
                    act.wait_ge(s_ctb, g * NC + (k + 1))
                    if k == 0 and not is_first(g):
                        act.wait_ge(s_kv, g * (NC + GB))
                    sc.activation(ctxT(HI, k), xaff[:, k % 2, 0:GN], ACT.Copy).then_inc(s_cthi, 1)
                for c in range(NC):
                    act.wait_ge(s_kv, g * (NC + GB) + (c + 1))
                    if c >= 2 or not is_first(g):
                        act.wait_ge(s_kst_out[c % 2], g * 64 + (c // 2) * 32)
                    sc.activation(qT[:, c % 2, HI, 0:GN], KVB[c][:, 0:GN], ACT.Identity, bias=vecs[:, 20 + c:21 + c])\
                      .then_inc(s_khi, 1)

            group(0)
            with act.Fori(1, NG) as g:
                group(g)

            def step(t):
                if t.has(-2):
                    t.wait(act, u_onorm, -2)
                    t.wait(act, u_out, -7)
                    sc.activation(outT[:, HI, (t.k - 2) % (2 * NC), :], onorm[:, t.k % 2, :], ACT.Copy)\
                      .then_inc(u_ohi, 1)
                if t.has(1):
                    par = (t.k + 1) % 2
                    t.wait(act, u_qproj, 1)
                    t.wait(act, u_smax, -1)
                    t.wait_ring(act, s_qst, -1, 3 * HG)
                    sc.activation(qT[:, par, HI, :], pA[:, :], ACT.Identity, bias=vecs[:, 16 + t.chunk(1):17 + t.chunk(1)])\
                      .then_inc(u_qhi, 1)
                if t.has(-1):
                    t.wait(act, u_st, -1)
                    t.wait(act, u_av, -3)
                    sc.activation(probs[0:KV, (t.k - 1) % 2], S[0:KV, :, :], ACT.Exp, scale=SCALE).then_inc(u_exp, 1)
                if t.has(0):
                    t.wait(act, u_mt, 0)
                    t.wait_ring(act, s_mst, -2)
                    sc.activation(mT[:, t.k % 2, :], pA[0:2 * HG, :], ACT.Copy).then_inc(u_mtc, 1)
                w = XT_AHEAD
                if t.has(w):
                    par, k = ((t.k + w) // NC) % 2, t.chunk(w)
                    t.wait(act, u_xt, w)
                    t.wait_batch(act, b_aff, w)
                    t.wait_units_of_batch(act, u_qproj, w, back=2)
                    t.wait(act, u_xlo, w - 2)
                    for dst in (xT[:, HI, par, k, :], xaff[:, (t.k + w) % 2, :]):
                        last = sc.activation(dst, pB[:, :], ACT.Identity, bias=affb[:, par, NC + k:NC + k + 1],
                                             scale=affb[:, par, k:k + 1])
                    last.then_inc(u_xaff, 1)

            steps(act, step)

        @block.vector
        def _(dve):
            ve = nc.vector
            ve.memset(minus_half[:, :], -0.5)
            ve.memset(eps4[:, :], EPS)
            ve.memset(one_zero[:, 0:NC], 1.0)
            ve.memset(one_zero[:, NC:2 * NC], 0.0)
            for par in range(2):
                ve.memset(f(kst[3 * DH:KS, par]), 1.0)
            ve.memset(ones[:, :], 1.0).then_inc(s_const, 1)
            dve.wait_ge(s_cexp, 1)
            ve.tensor_scalar(cexp[:, :], cexp[:, :], 1.0, None, ALU.add).then_inc(s_cden, 1)
            dve.wait_ge(s_cden, 1)
            ve.reciprocal(cexp[:, :], cexp[:, :]).then_inc(s_crec, 1)
            dve.wait_ge(s_crec, 1)
            ve.tensor_tensor(csilu[:, :], crow[:, :], cexp[:, :], ALU.mult).then_inc(s_silu, 1)
            dve.wait_ge(s_early, 1)
            ve.tensor_copy(csT[:, :, :], pA[:, 0:NC * NB].rearrange("p (k b) -> p k b", k=NC))
            ve.tensor_copy(vecs[:, :], pA[:, 256:256 + 24]).then_inc(s_earlyc, 1)
            lo = [outT[:, LO, 0:NC], outT[:, LO, NC:2 * NC], wq[:, LO], wp[:, LO]]
            hi = [outT[:, HI, 0:NC], outT[:, HI, NC:2 * NC], wq[:, HI], wp[:, HI]]

            def split_weight(n):
                dve.wait_ge(s_whi, n + 1)
                ve.tensor_tensor(lo[n], xin[:, n % 2], f(hi[n]), ALU.subtract).then_inc(s_wlo, 1)

            split_weight(0)
            split_weight(1)
            dve.wait_ge(s_earlyc, 1)
            for n in range(2):
                dve.wait_ge(s_ss, n + 1)
                ve.tensor_tensor(aff[n][:, :, :], (pB, pV)[n][:, 0:2 * NC * NB].rearrange("p (m b) -> p m b", b=NB),
                                 vecs[:, 8 * n:8 * n + 8].rearrange("p (m a) -> p m a", a=1)
                                 .broadcast_to([P, 2 * NC, NB]), ALU.add).then_inc(s_ssb, 1)
            split_weight(2)
            split_weight(3)
            dve.wait_ge(s_bcast, 32)

            def ctx_stats(g):
                dve.wait_ge(s_ctx, g * 16 + 16)
                for b in range(GB):
                    last = ve.bn_stats(bst[0:KV, b, :], cin[:, b, :])
                last.then_inc(s_cst, 1)

            def ctx_aggr():
                for b in range(GB):
                    last = ve.bn_aggr(mv[0:KV, 0, b, :], bst[0:KV, b, :])
                last.then_inc(s_cag, 1)

            def ctx_normalise(g):
                dve.wait_ge(s_crs, g + 1)
                if not is_first(g):
                    dve.wait_ge(s_ct, g * NC)
                for b in range(GB):
                    last = ve.tensor_scalar(hctx[:, b, :], cin[:, b, :], mv[0:KV, 0, b, 0:1], rstd[0:KV, 0, b:b + 1],
                                            ALU.subtract, ALU.mult)
                last.then_inc(s_hctx, 1)

            def ctx_scale(g):
                for k in range(NC):
                    dve.wait_ge(s_ct, g * NC + (k + 1))
                    if k >= 2:
                        dve.wait_ge(s_ctlo, g * NC + (k - 1))
                    scale = aff[0][:, k, bass.ds(g * GB, GB)].rearrange("p (b a) -> p b a", a=1)\
                        .broadcast_to([P, GB, KV])
                    ve.tensor_tensor(xaff[:, k % 2, 0:GN].rearrange("p (b t) -> p b t", b=GB),
                                     S[:, k, 0:GN].rearrange("p (b t) -> p b t", b=GB), scale, ALU.mult)\
                      .then_inc(s_ctm, 1)

            def k_lo(g):
                for c in range(NC):
                    dve.wait_ge(s_khi, g * NC + (c + 1))
                    ve.scalar_tensor_tensor(out=qT[:, c % 2, LO, 0:GN], in0=KVB[c][:, 0:GN],
                                            scalar=vecs[:, 20 + c:21 + c], in1=f(qT[:, c % 2, HI, 0:GN]),
                                            op0=ALU.add, op1=ALU.subtract).then_inc(s_kvout, 1)

            def v_out(g):
                for b in range(GB):
                    dve.wait_ge(s_kv, g * (NC + GB) + (NC + b + 1))
                    if b >= 2 or not is_first(g):
                        dve.wait_ge(s_v_out[b % 2], g * 32 + (b // 2) * 16)
                    ve.tensor_tensor(onorm[0:KV, b % 2, :], KVB[b][0:KV, :], bv_bc[0:KV, :], ALU.add)\
                      .then_inc(s_kvout, 1)

            ctx_stats(0)
            dve.wait_ge(s_cst, 1)
            ctx_aggr()
            ctx_normalise(0)
            dve.wait_ge(s_aff, 1)

            def group(g):
                ctx_scale(g)
                ctx_stats(g + 1)
                dve.wait_ge(s_cst, g + 2)
                k_lo(g)
                ctx_aggr()
                ctx_normalise(g + 1)
                v_out(g)

            group(0)
            with dve.Fori(1, NG - 1) as g:
                group(g)
            ctx_scale(NG - 1)
            k_lo(NG - 1)
            v_out(NG - 1)

            def step(t):
                if t.has(-2):
                    t.wait(dve, u_av, -2)
                    ve.reciprocal(rsum[:, :], pD[:, :]).then_inc(u_rsum, 1)
                    t.wait(dve, u_rsum, -2)
                    t.wait(dve, u_olo, -4)
                    ve.tensor_tensor(onorm[:, t.k % 2, :], pV[:, :], rsum[:, :], ALU.mult).then_inc(u_onorm, 1)
                if t.has(0):
                    t.wait(dve, u_smax, 0)
                    ve.tensor_reduce(out=mneg[:, :, :],
                                     in_=S[:, :, 0:HG * KV].rearrange("p t (j n) -> p t j n", j=HG),
                                     axis=AX.X, op=ALU.max, negate=True).then_inc(u_mneg, 1)
                    t.wait(dve, u_mneg, 0)
                    t.wait(dve, u_mt, -1)
                    ve.tensor_copy(mhl[:, :, 0:HG], mneg[:, :, :]).then_inc(u_mhi, 1)
                    t.wait(dve, u_mhi, 0)
                    ve.tensor_tensor(mhl[:, :, HG:2 * HG], mneg[:, :, :], f(mhl[:, :, 0:HG]), ALU.subtract)\
                      .then_inc(u_msplit, 1)
                if t.has(1):
                    par, c = (t.k + 1) % 2, t.chunk(1)
                    t.wait(dve, u_qhi, 1)
                    ve.scalar_tensor_tensor(out=qT[:, par, LO, :], in0=pA[:, :], scalar=vecs[:, 16 + c:17 + c],
                                            in1=f(qT[:, par, HI, :]), op0=ALU.add, op1=ALU.subtract)\
                      .then_inc(u_qlo, 1)
                d = XT_AHEAD
                if t.has(d) and t.chunk(d) == 0:
                    par = ((t.k + d) // NC) % 2
                    t.wait_batch(dve, b_rstd, d)
                    t.wait(dve, u_xt, d - 1)
                    for tt in range(NT):
                        last = ve.tensor_scalar(h[:, tt, :], xin[:, par, tt, :], mv[:, par, tt, 0:1],
                                                rstd[:, par, tt:tt + 1], ALU.subtract, ALU.mult)
                    last.then_inc(b_h, 1)
                d = XT_AHEAD + 1
                new_batch, par = t.has(d) and t.chunk(d) == 0, ((t.k + d) // NC) % 2
                if new_batch:
                    t.wait_batch_dma(dve, s_x, d)
                    for tt in range(NT):
                        last = ve.bn_stats(bst[:, tt, :], xin[:, par, tt, :])
                    last.then_inc(b_stats, 1)
                    t.wait_batch(dve, b_stats, d)
                    ve.tensor_tensor(affb[:, par, :], one_zero[:, :],
                                     aff[1][:, :, bass.ds(t.batch(d), 1)].rearrange("p c a -> p (c a)"), ALU.add)\
                      .then_inc(b_aff, 1)
                    for tt in range(NT):
                        last = ve.bn_aggr(mv[:, par, tt, :], bst[:, tt, :])
                    last.then_inc(b_aggr, 1)
                if t.has(-OUT_BEHIND):
                    slot = (t.k - OUT_BEHIND) % 4
                    t.wait(dve, u_out, -OUT_BEHIND)
                    t.wait(dve, u_resb, -OUT_BEHIND)
                    ve.tensor_tensor(xres[:, slot, :], pB[:, :], xres[:, slot, :], ALU.add).then_inc(u_y, 1)

            steps(dve, step)

        @block.tensor
        def _(pe):
            te = nc.tensor
            pe.wait_ge(s_ident, 2)
            pe.wait_ge(s_const, 1)
            pe.wait_ge(s_silu, 1)
            for k in range(NC):
                te.transpose(pA[:, k * NB:(k + 1) * NB], csilu[:, k * P:(k + 1) * P], ident[0:NB, 0:NB])
            pe.wait_ge(s_vecrows, 64)
            te.transpose(pA[:, 256:256 + 24], vecrows[:, :], ident[0:24, 0:24]).then_inc(s_early, 1)
            pe.wait_ge(s_earlyc, 1)
            for n in range(2):
                pe.wait_ge(s_wss[n], 16)
                for m in range(2 * NC):
                    for k in range(NC):
                        last = te.matmul((pB, pV)[n][:, m * NB:(m + 1) * NB], wss[n][:, k, m * P:(m + 1) * P],
                                         csT[:, k, :], start=(k == 0), stop=(k == NC - 1))
                last.then_inc(s_ss, 1)
            pe.wait_ge(s_ssb, 2)

            def group(g):
                for k in range(NC):
                    if k == 0:
                        pe.wait_ge(s_hctx, g + 1)
                    if not is_first(g):
                        pe.wait_ge(s_ctm, g * NC + k)
                    for b in range(GB):
                        last = te.transpose(S[:, k, b * KV:(b + 1) * KV], hctx[:, b, k * P:(k + 1) * P],
                                            ident[0:KV, 0:KV])
                    last.then_inc(s_ct, 1)
                pe.wait_ge(s_wlo, 2)
                for c in range(NC):
                    if not is_first(g):
                        pe.wait_ge(s_kvout, g * (NC + GB))
                    n = 0
                    for k in range(NC):
                        if c == 0:
                            pe.wait_ge(s_ctlo, g * NC + (k + 1))
                        for wl, xl in PASSES:
                            last = te.matmul(KVB[c][:, 0:GN], wk(wl, k)[:, c * P:(c + 1) * P], ctxT(xl, k),
                                             start=(n == 0), stop=(n == 3 * NC - 1))
                            n += 1
                    last.then_inc(s_kv, 1)
                for b in range(GB):
                    pe.wait_ge(s_kvout, g * (NC + GB) + (b + 1))
                    n = 0
                    for k in range(NC):
                        for xl, wl in PASSES:
                            last = te.matmul(KVB[b][0:KV, :], ctxT(xl, k)[:, b * KV:(b + 1) * KV], wv(wl, k),
                                             start=(n == 0), stop=(n == 3 * NC - 1))
                            n += 1
                    last.then_inc(s_kv, 1)

            group(0)
            with pe.Fori(1, NG) as g:
                group(g)
            pe.wait_ge(s_wlo, 4)

            def step(t):
                if t.has(0):
                    par = t.k % 2
                    t.wait(pe, u_qhi, 0)
                    t.wait(pe, u_kbd, 0)
                    t.wait(pe, u_exp, -2)
                    for tt in range(NT):
                        last = te.matmul(S[:, tt, 0:HG * KV], qT[:, par, HI, tt * P:(tt + 1) * P],
                                         kbd[:, par].rearrange("p j n -> p (j n)"), start=True, stop=True)
                    last.then_inc(u_smax, 1)
                if t.has(1):
                    c, bpar = t.chunk(1), ((t.k + 1) // NC) % 2
                    if c == 0:
                        t.wait_units_of_batch(pe, u_xlo, 1)
                    t.wait(pe, u_mtc, -1)
                    if t.static and t.i == 0 and t.k == -1:
                        pe.wait_ge(s_kvout, NG * (NC + GB))
                    n = 0
                    for k in range(NC):
                        for wl, xl in PASSES:
                            last = te.matmul(pA[:, :], wq[:, wl, k, c * P:(c + 1) * P], xT[:, xl, bpar, k, :],
                                             start=(n == 0), stop=(n == 3 * NC - 1))
                            n += 1
                    last.then_inc(u_qproj, 1)
                if t.has(-1):
                    par = (t.k - 1) % 2
                    t.wait_ring(pe, s_kst, -1, 3)
                    t.wait_ring(pe, s_qst, -1, 3 * HG)
                    t.wait_ring(pe, s_mst, -1)
                    t.wait(pe, u_mneg, 0)
                    for j in range(HG):
                        last = te.matmul(S[0:KV, j, :], kst[0:KS, par, j, :], stack[0:KS, par, j, :],
                                         start=True, stop=True)
                    last.then_inc(u_st, 1)
                if t.has(-OUT_BEHIND):
                    tt, half = t.chunk(-OUT_BEHIND), ((t.k - OUT_BEHIND) // NC) % 2 * NC
                    if tt == 0:
                        t.wait_units_of_batch(pe, u_olo, -OUT_BEHIND)
                    t.wait(pe, u_xaff, XT_AHEAD - 1)
                    if not t.has(XT_AHEAD - 1):
                        t.wait(pe, u_y, -OUT_BEHIND - 1)
                    n = 0
                    for k in range(NC):
                        for xl, wl in PASSES:
                            last = te.matmul(pB[:, :], outT[:, xl, half + k, tt * P:(tt + 1) * P], wp[:, wl, k, :],
                                             start=(n == 0), stop=(n == 3 * NC - 1))
                            n += 1
                    last.then_inc(u_out, 1)
                if t.has(0):
                    t.wait(pe, u_msplit, 0)
                    t.wait(pe, u_qlo, 1)
                    if not t.has(1):
                        t.wait(pe, u_mtc, -1)
                    for tt in range(NT):
                        last = te.transpose(pA[0:2 * HG, tt * P:(tt + 1) * P], f(mhl[:, tt, :]), ident[:, :])
                    last.then_inc(u_mt, 1)
                if t.has(-1):
                    par, bpar, c = (t.k - 1) % 2, ((t.k - 1) // NC) % 2, t.chunk(-1)
                    t.wait(pe, u_exp, -1)
                    t.wait_batch_dma(pe, s_v, -1)
                    t.wait(pe, u_onorm, -2)
                    for j in range(HG):
                        te.matmul(pV[DH * j:DH * (j + 1), :], vt[0:KV, bpar, (c * HG + j) * DH:(c * HG + j + 1) * DH],
                                  probs[0:KV, par, j, :], start=True, stop=True)
                    for j in range(HG):
                        last = te.matmul(pD[DH * j:DH * (j + 1), :], ones[0:KV, :], probs[0:KV, par, j, :],
                                         start=True, stop=True)
                    last.then_inc(u_av, 1)
                w = XT_AHEAD
                if t.has(w):
                    k = t.chunk(w)
                    if k == 0:
                        t.wait_batch(pe, b_h, w)
                    t.wait(pe, u_y, -OUT_BEHIND)
                    t.wait(pe, u_xaff, w - 1)
                    for tt in range(NT):
                        last = te.transpose(pB[:, tt * P:(tt + 1) * P], h[:, tt, k * P:(k + 1) * P], ident[:, :])
                    last.then_inc(u_xt, 1)

            steps(pe, step)


_INS = ["x", "ctx_1024", "cond_1024", "L0_xcond_Wq", "L0_xcond_bq", "L0_xcond_Wkv", "L0_xcond_bkv", "L0_xcond_Wp",
        "L0_xcond_bp", "L0_xcond_Wss_q", "L0_xcond_bss_q", "L0_xcond_Wss_kv", "L0_xcond_bss_kv"]
_OUT = ((16, 512, 512), "float32")


def kernel(**inputs):
    import numpy as _np
    import concourse.bacc as _bacc
    from concourse import mybir as _mybir
    from concourse.bass_utils import run_bass_kernel_spmd as _run

    nc = _bacc.Bacc("TRN2", target_bir_lowering=False, num_devices=1)
    arrays, args = {}, []
    for name in _INS:
        a = _np.ascontiguousarray(inputs[name])
        arrays[f"in_{name}_dram"] = a
        args.append(nc.dram_tensor(f"in_{name}_dram", a.shape, _mybir.dt.from_np(a.dtype), kind="ExternalInput").ap())
    shape, dtype = _OUT
    args.append(nc.dram_tensor("out_0_dram", shape, _mybir.dt.from_np(_np.dtype(dtype)), kind="ExternalOutput").ap())
    adaln_cross_attention_kernel(nc, *args)
    r = _run(nc, [arrays], core_ids=[0])
    return r.results[0]["out_0_dram"]
```

```python
import concourse.bass as bass
from concourse import mybir
from contextlib import ExitStack


def adaln_cross_attention_kernel(
    nc: bass.Bass,
    x: bass.AP,
    ctx_kv: bass.AP,
    cond: bass.AP,
    Wq: bass.AP,
    bq: bass.AP,
    Wkv: bass.AP,
    bkv: bass.AP,
    Wp: bass.AP,
    bp: bass.AP,
    Wss_q: bass.AP,
    bss_q: bass.AP,
    Wss_kv: bass.AP,
    bss_kv: bass.AP,
    out: bass.AP,
):
    f32, f32r = mybir.dt.float32, mybir.dt.float32r
    ALU, ACT, AX = mybir.AluOpType, mybir.ActivationFunctionType, mybir.AxisListType

    P = 128
    NB, L, D = x.shape
    KV = ctx_kv.shape[1]
    NH = 16
    DH = D // NH
    NC = D // P
    NT = L // P
    HG = P // DH
    EPS = 1e-5
    SCALE = float(DH) ** -0.5
    UNITS = NB * NC
    PAIR = 2 * NC
    GB = 4
    NG = NB // GB
    GN = GB * KV
    KS = 3 * DH + 1
    Q_AHEAD, XT_AHEAD, OUT_BEHIND = 2, 7, 6
    HI, LO = 0, 1
    PASSES = ((HI, HI), (HI, LO), (LO, HI))
    X_AHEAD = XT_AHEAD + 2
    assert NC == NT == HG == 4 and 3 * DH == 96

    x_tiles = x.rearrange("b (t p) n -> (b t) p n", p=P)
    out_tiles = out.rearrange("b (t p) n -> (b t) p n", p=P)
    k_scratch = nc.dram_tensor("k_scratch", [NC, HG, 3 * DH, 1 + NB, KV], f32, kind="Internal").ap()[:, :, :, 1:, :]
    v_scratch = nc.dram_tensor("v_scratch", [NB, KV, D], f32, kind="Internal").ap()

    ctx = ExitStack()
    with ctx:
        def sb(name, shape, dt=f32, where=ctx):
            return where.enter_context(nc.sbuf_tensor(name, shape, dt))

        def sem(name):
            return ctx.enter_context(nc.semaphore(name))

        with ExitStack() as early:
            wss = [sb("wss_kv", [P, NC, 2 * D], f32, early), sb("wss_q", [P, NC, 2 * D], f32, early)]
        xT = sb("xT", [P, 2, 2, NC, L], f32r)
        wq = sb("wq", [P, 2, NC, D], f32r)
        wp = sb("wp", [P, 2, NC, D], f32r)
        outT = sb("outT", [P, 2, 2 * NC, L], f32r)
        stack = sb("stack", [P, 2, 2, HG, L], f32r)
        qT = sb("qT", [P, 2, 2, 2, L], f32r)
        xin = sb("xin", [P, NT, D])
        xres = sb("xres", [P, 4, D])
        h = sb("h", [P, NT, D])
        probs = sb("probs", [P, HG, L])
        onorm = sb("onorm", [P, 2, L])
        rsum = sb("rsum", [P, L])
        xaff = sb("xaff", [P, 2, L])
        kst = sb("kst", [P, 2, HG, KV], f32r)
        kh = sb("kh", [P, 2, KV], f32r)
        kbd = sb("kbd", [P, 2, HG, KV], f32r)
        vt = sb("vt", [P, 2, D])
        bp_bc = sb("bp_bc", [P, D])
        ident = sb("ident", [P, P])
        ones = sb("ones", [P, DH])
        headmask = sb("headmask", [P, HG])
        minus_half = sb("minus_half", [P, 4])
        eps4 = sb("eps4", [P, 4])
        vecrows = sb("vecrows", [24, P])
        vecs = sb("vecs", [P, 24])
        csT = sb("csT", [P, NC, NB])
        aff = [sb("aff_kv", [P, 2 * NC, NB]), sb("aff_q", [P, 2 * NC, NB])]
        one_zero = sb("one_zero", [P, 2 * NC])
        affb = sb("affb", [P, 2, 2 * NC])
        bst = sb("bst", [P, 4, 6])
        mv = sb("mv", [P, 2, 4, 2])
        rstd = sb("rstd", [P, 2, 4])
        mneg = sb("mneg", [P, NT, HG], f32r)
        mT = sb("mT", [HG, 2, L], f32r)

        def wk(hl, k):
            return outT[:, hl, k, :]

        def wv(hl, k):
            return outT[:, hl, NC + k, :]

        def ctxT(hl, k):
            return stack[:, 0, hl, k, 0:GN]

        hctx, cin = probs[0:KV], xres[0:KV]
        staging = (xin, h)
        crow, cexp = vt[0:NB, 0, :], vt[0:NB, 1, :]
        csilu, bv_bc = xaff[0:NB, 0, :], rsum

        def f(ap):
            return ap.bitcast(f32)

        S = ctx.enter_context(nc.psum_tensor("S", [P, 4, 512], f32))
        pA = ctx.enter_context(nc.psum_tensor("pA", [P, 512], f32))
        pB = ctx.enter_context(nc.psum_tensor("pB", [P, 512], f32))
        pV = ctx.enter_context(nc.psum_tensor("pV", [P, 512], f32))
        pD = ctx.enter_context(nc.psum_tensor("pD", [P, 512], f32))
        KVB = (pA, pB, pV, pD)

        s_wss = [sem("s_wss_kv_in"), sem("s_wss_q_in")]
        s_cond, s_vecrows, s_bcast = sem("s_cond_in"), sem("s_vecrows_in"), sem("s_bcast_in")
        s_win = [sem(f"s_weight_in{n}") for n in range(4)]
        s_ctx = sem("s_ctx_in")
        s_const, s_ident, s_mask = sem("s_const"), sem("s_ident"), sem("s_mask")
        s_cexp, s_cden, s_crec, s_silu = sem("s_cexp"), sem("s_cden"), sem("s_crec"), sem("s_silu")
        s_early, s_earlyc = sem("s_early_transposed"), sem("s_early_copied")
        s_ss, s_ssb, s_aff = sem("s_ss"), sem("s_ss_biased"), sem("s_aff")
        s_whi, s_wlo = sem("s_weight_hi"), sem("s_weight_lo")
        s_cst, s_cag, s_cve, s_crs = sem("s_ctx_stats"), sem("s_ctx_aggr"), sem("s_ctx_vareps"), sem("s_ctx_rstd")
        s_hctx = sem("s_ctx_normalised")
        s_ct, s_ctm, s_ctb, s_cthi, s_ctlo = (sem("s_ctxT"), sem("s_ctxT_scaled"), sem("s_ctxT_biased"),
                                              sem("s_ctxT_hi"), sem("s_ctxT_lo"))
        s_kv, s_kvout, s_khi = sem("s_kv_product"), sem("s_kv_evacuated"), sem("s_k_hi")
        s_kst_out = [sem("s_k_stored0"), sem("s_k_stored1")]
        s_v_out = [sem("s_v_stored0"), sem("s_v_stored1")]
        s_x = sem("s_x_in")
        s_xres = [sem(f"s_xres_in{n}") for n in range(4)]
        s_store = [sem(f"s_y_stored{n}") for n in range(4)]
        s_kst = [sem("s_kst_in0"), sem("s_kst_in1")]
        s_kh = [sem("s_kh_in0"), sem("s_kh_in1")]
        s_v = [sem("s_v_in0"), sem("s_v_in1")]
        s_qst = [sem("s_qstack_in0"), sem("s_qstack_in1")]
        s_mst = [sem("s_mstack_in0"), sem("s_mstack_in1")]
        (u_qproj, u_qhi, u_qlo, u_kbd, u_smax, u_mneg, u_mt, u_mtc, u_st, u_exp, u_av, u_lnsum, u_rsum, u_rerr,
         u_onorm, u_ohi, u_olo, u_out, u_resb, u_y, u_xt, u_xaff, u_xlo) = (sem("u_" + n) for n in (
            "qproj qhi qlo kbd smax mneg mt mtcopied st exp av lnsum rsum rerr onorm outhi outlo out "
            "resbiased y xt xaff xlo").split())
        b_stats, b_aggr, b_vareps, b_rstd, b_h, b_aff = (sem("b_" + n) for n in
                                                         "stats aggr vareps rstd h aff".split())

        block = ctx.enter_context(nc.Block())

        def is_first(g):
            return isinstance(g, int) and g == 0

        class Step:

            def __init__(self, i, k):
                self.i, self.k = i, k
                self.static = isinstance(i, int)

            def has(self, d):
                return not self.static or 0 <= PAIR * self.i + self.k + d < UNITS

            def unit(self, d):
                return self.i * PAIR + (self.k + d)

            def batch(self, d):
                return self.i * 2 + (self.k + d) // NC

            def chunk(self, d):
                return (self.k + d) % NC

            def wait(self, eng, s, d, per=1, base=0):
                if not self.static:
                    eng.wait_ge(s, self.i * (PAIR * per) + ((self.k + d + 1) * per + base))
                    return
                n = min(PAIR * self.i + self.k + d + 1, UNITS)
                if n > 0:
                    eng.wait_ge(s, n * per + base)

            def wait_batch(self, eng, s, d, back=0):
                if not self.static:
                    eng.wait_ge(s, self.i * 2 + ((self.k + d) // NC + 1 - back))
                    return
                n = (PAIR * self.i + self.k + d) // NC + 1 - back
                if n > 0:
                    eng.wait_ge(s, n)

            def wait_units_of_batch(self, eng, s, d, back=0):
                if not self.static:
                    eng.wait_ge(s, self.i * PAIR + ((self.k + d) // NC + 1 - back) * NC)
                    return
                n = ((PAIR * self.i + self.k + d) // NC + 1 - back) * NC
                if n > 0:
                    eng.wait_ge(s, n)

            def wait_ring(self, eng, sems, d, dmas=1):
                m = len(sems)
                s = sems[(self.k + d) % m]
                if not self.static:
                    eng.wait_ge(s, self.i * (PAIR // m * 16 * dmas) + ((self.k + d) // m + 1) * 16 * dmas)
                    return
                n = (PAIR * self.i + self.k + d) // m + 1
                if n > 0:
                    eng.wait_ge(s, n * 16 * dmas)

            def wait_pair(self, eng, sems, d, dmas):
                m = (self.k + d) // 2
                n = PAIR // 4 * self.i + m // 2 + 1
                if not self.static or n > 0:
                    eng.wait_ge(sems[m % 2], n * (16 * dmas))

            def wait_batch_dma(self, eng, sems, d):
                bk = (self.k + d) // NC
                if not self.static:
                    eng.wait_ge(sems[bk % 2], self.i * 16 + (bk // 2 + 1) * 16)
                    return
                eng.wait_ge(sems[bk % 2], ((2 * self.i + bk) // 2 + 1) * 16)

        def steps(eng, step):
            for k in range(-X_AHEAD, PAIR - 1):
                step(Step(0, k))
            with eng.Fori(1, NB // 2 - 1) as i:
                for k in range(-1, PAIR - 1):
                    step(Step(i, k))
            for k in range(-1, PAIR + OUT_BEHIND):
                step(Step(NB // 2 - 1, k))

        @block.sync
        def _(sp):
            sp.dma_start(crow, cond).then_inc(s_cond, 16)
            for row, src in ((0, bss_kv), (8, bss_q), (16, bq), (20, bkv[0:D])):
                n = src.shape[0] // P
                sp.dma_start(vecrows[row:row + n, :], src.rearrange("(a n) -> a n", n=P)).then_inc(s_vecrows, 16)
            sp.dma_start(wss[0][:, :, :], Wss_kv.rearrange("(k p) n -> p k n", p=P)).then_inc(s_wss[0], 16)
            sp.dma_start(cin, ctx_kv[0:GB].rearrange("b t n -> t b n")).then_inc(s_ctx, 16)
            weights = [Wkv[:, 0:D], Wkv[:, D:2 * D], Wq, Wp]
            for n in range(2):
                sp.dma_start(staging[n][:, :, :], weights[n].rearrange("(k p) n -> p k n", p=P)).then_inc(s_win[n], 16)
            sp.dma_start(wss[1][:, :, :], Wss_q.rearrange("(k p) n -> p k n", p=P)).then_inc(s_wss[1], 16)
            sp.dma_start(bp_bc[:, :], bp.rearrange("(a n) -> a n", a=1).broadcast_to([P, D])).then_inc(s_bcast, 16)
            sp.dma_start(bv_bc[:, :], bkv[D:2 * D].rearrange("(a n) -> a n", a=1).broadcast_to([P, D])).then_inc(s_bcast, 16)
            for n in range(2, 4):
                sp.wait_ge(s_whi, n - 1)
                sp.wait_ge(s_wlo, n - 1)
                sp.dma_start(staging[n - 2][:, :, :], weights[n].rearrange("(k p) n -> p k n", p=P)).then_inc(s_win[n], 16)

            def store_group(g):
                for c in range(NC):
                    sp.wait_ge(s_kvout, g * (NC + GB) + (c + 1))
                    for s, hl in enumerate((HI, LO, HI)):
                        sp.dma_start(k_scratch[c, :, DH * s:DH * (s + 1), bass.ds(g * GB, GB), :], f(qT[:, 0, c % 2, hl, 0:GN]))\
                          .then_inc(s_kst_out[c % 2], 16)
                for b in range(GB):
                    sp.wait_ge(s_kvout, g * (NC + GB) + (NC + b + 1))
                    sp.dma_start(v_scratch[bass.ds(g * GB + b, 1)].rearrange("a t n -> (a t) n"), onorm[0:KV, b % 2, :])\
                      .then_inc(s_v_out[b % 2], 16)

            with sp.Fori(0, NG - 1) as g:
                sp.wait_ge(s_hctx, g + 1)
                sp.dma_start(cin, ctx_kv[bass.ds(g * GB + GB, GB)].rearrange("b t n -> t b n")).then_inc(s_ctx, 16)
                store_group(g)
            store_group(NG - 1)
            for par in range(2):
                sp.wait_ge(s_kst_out[par], 16 * 3 * NG * NC // 2)
                sp.wait_ge(s_v_out[par], 16 * NG * GB // 2)

            def step(t):
                d = X_AHEAD
                if t.chunk(d) == 0 and t.has(d):
                    if t.static and PAIR * t.i + t.k + d == 0:
                        sp.wait_ge(s_whi, 4)
                        sp.wait_ge(s_wlo, 4)
                    t.wait_batch(sp, b_h, d, back=1)
                    sp.dma_start(xin[:, :, :], x[bass.ds(t.batch(d), 1)].rearrange("a (t p) n -> p (a t) n", p=P))\
                      .then_inc(s_x, 16)
                if t.chunk(2) == 0 and t.has(2):
                    t.wait_units_of_batch(sp, u_av, 2, back=2)
                    par = ((t.k + 2) // NC) % 2
                    sp.dma_start(vt[0:KV, par, :], v_scratch[bass.ds(t.batch(2), 1)].rearrange("a t n -> (a t) n"))\
                      .then_inc(s_v[par], 16)
                if t.has(2):
                    t.wait(sp, u_kbd, 0)
                    sp.dma_start(f(kh[:, t.k % 2, :]), k_scratch[t.chunk(2), :, 0:DH, bass.ds(t.batch(2), 1), :])\
                      .then_inc(s_kh[t.k % 2], 16)
                if t.has(1):
                    par = (t.k + 1) % 2
                    t.wait(sp, u_st, -1)
                    sp.dma_start(f(kst[0:3 * DH, par]),
                                 k_scratch[t.chunk(1), :, :, bass.ds(t.batch(1), 1), :]
                                 .rearrange("j r b n -> r j (b n)")).then_inc(s_kst[par], 16)
                q = Q_AHEAD
                if t.has(q) and (t.k + q) % 2:
                    par = ((t.k + q) // 2) % 2
                    t.wait(sp, u_qlo, q)
                    for s, hl in enumerate((HI, HI, LO)):
                        for j in range(HG):
                            sp.dma_start(f(stack[DH * s:DH * (s + 1), par, :, j, :]),
                                         f(qT[DH * j:DH * (j + 1), par, :, hl, :])).then_inc(s_qst[par], 16)
                if t.has(-OUT_BEHIND):
                    t.wait(sp, u_y, -OUT_BEHIND)
                    slot = (t.k - OUT_BEHIND) % 4
                    sp.dma_start(out_tiles[bass.ds(t.unit(-OUT_BEHIND), 1)].rearrange("a p n -> (a p) n"),
                                 xres[:, slot, :]).then_inc(s_store[slot], 16)
                if t.has(-3):
                    if not (t.static and PAIR * t.i + t.k - 3 < 4):
                        t.wait_ring(sp, s_store, -7)
                    slot = (t.k - 3) % 4
                    sp.dma_start(xres[:, slot, :],
                                 x_tiles[bass.ds(t.unit(-3), 1)].rearrange("a p n -> (a p) n")).then_inc(s_xres[slot], 16)

            steps(sp, step)
            for s in s_store:
                sp.wait_ge(s, 16 * UNITS // 4)

        @block.gpsimd
        def _(pool):
            gp = nc.gpsimd
            gp.memset(ident[:, :], 0.0).then_inc(s_ident, 1)
            pool.wait_ge(s_ident, 1)
            gp.affine_select(out=ident[:, :], in_=ident[:, :], compare_op=ALU.not_equal, fill=1.0, base=0,
                             pattern=[[-1, P]], channel_multiplier=1).then_inc(s_ident, 1)
            pool.wait_ge(s_ident, 2)
            gp.memset(headmask[:, :], 1.0).then_inc(s_mask, 1)
            pool.wait_ge(s_mask, 1)
            gp.affine_select(out=headmask[:, :], in_=headmask[:, :], compare_op=ALU.is_ge, fill=0.0, base=0,
                             pattern=[[-DH, HG]], channel_multiplier=1).then_inc(s_mask, 1)
            pool.wait_ge(s_mask, 2)
            gp.affine_select(out=headmask[:, :], in_=headmask[:, :], compare_op=ALU.is_ge, fill=0.0, base=DH - 1,
                             pattern=[[DH, HG]], channel_multiplier=-1).then_inc(s_mask, 1)
            pool.wait_ge(s_mask, 3)
            pool.wait_ge(s_const, 1)
            pool.wait_ge(s_ssb, 1)
            gp.tensor_scalar(aff[0][:, 0:NC, :], aff[0][:, 0:NC, :], 1.0, None, ALU.add).then_inc(s_aff, 1)
            pool.wait_ge(s_aff, 1)
            with pool.Fori(0, NG) as g:
                pool.wait_ge(s_cag, g + 1)
                gp.tensor_tensor(rstd[0:KV, 0, :], mv[0:KV, 0, :, 1], eps4[0:KV, :], ALU.add).then_inc(s_cve, 1)
                pool.wait_ge(s_cve, g + 1)
                gp.tensor_tensor(rstd[0:KV, 0, :], rstd[0:KV, 0, :], minus_half[0:KV, :], ALU.pow).then_inc(s_crs, 1)
                for k in range(NC):
                    pool.wait_ge(s_cthi, g * NC + (k + 1))
                    gp.tensor_tensor(ctxT(LO, k), xaff[:, k % 2, 0:GN], f(ctxT(HI, k)), ALU.subtract)\
                      .then_inc(s_ctlo, 1)
            pool.wait_ge(s_bcast, 32)

            def step(t):
                if t.has(XT_AHEAD + 1) and t.chunk(XT_AHEAD + 1) == 0:
                    par = ((t.k + XT_AHEAD + 1) // NC) % 2
                    t.wait_batch(pool, b_aggr, XT_AHEAD + 1)
                    gp.tensor_tensor(rstd[:, par, :], mv[:, par, :, 1], eps4[:, :], ALU.add).then_inc(b_vareps, 1)
                    t.wait_batch(pool, b_vareps, XT_AHEAD + 1)
                    gp.tensor_tensor(rstd[:, par, :], rstd[:, par, :], minus_half[:, :], ALU.pow).then_inc(b_rstd, 1)
                w = XT_AHEAD - 1
                if t.has(w):
                    par, k = ((t.k + w) // NC) % 2, t.chunk(w)
                    t.wait(pool, u_xaff, w)
                    gp.tensor_tensor(xT[:, LO, par, k, :], xaff[:, (t.k + w) % 2, :], f(xT[:, HI, par, k, :]),
                                     ALU.subtract).then_inc(u_xlo, 1)
                if t.has(1):
                    par = (t.k + 1) % 2
                    t.wait_ring(pool, s_kh, 1)
                    t.wait(pool, u_smax, -1)
                    gp.tensor_tensor(kbd[:, par],
                                     f(kh[:, par, :]).rearrange("p (a n) -> p a n", a=1).broadcast_to([P, HG, KV]),
                                     headmask[:, :].rearrange("p (j a) -> p j a", a=1).broadcast_to([P, HG, KV]),
                                     ALU.mult).then_inc(u_kbd, 1)
                if t.has(-2):
                    t.wait(pool, u_ohi, -2)
                    gp.tensor_tensor(outT[:, LO, (t.k - 2) % (2 * NC), :], onorm[:, t.k % 2, :],
                                     f(outT[:, HI, (t.k - 2) % (2 * NC), :]), ALU.subtract).then_inc(u_olo, 1)
                if t.has(-5):
                    slot = (t.k - 5) % 4
                    t.wait_ring(pool, s_xres, -5)
                    gp.tensor_tensor(xres[:, slot, :], xres[:, slot, :], bp_bc[:, :], ALU.add).then_inc(u_resb, 1)

            steps(pool, step)

        @block.scalar
        def _(act):
            sc = nc.scalar
            sc.preload_act_table_set("natural_log_exp_and_others")
            act.wait_ge(s_cond, 16)
            sc.activation(cexp, crow, ACT.Exp, scale=-1.0).then_inc(s_cexp, 1)
            weights = [outT[:, HI, 0:NC], outT[:, HI, NC:2 * NC], wq[:, HI], wp[:, HI]]
            for n, hi in enumerate(weights):
                act.wait_ge(s_win[n], 16)
                sc.activation(hi, staging[n % 2][:, :, :], ACT.Copy).then_inc(s_whi, 1)

            def group(g):
                for k in range(NC):
                    act.wait_ge(s_ctb, g * NC + (k + 1))
                    if k == 0 and not is_first(g):
                        act.wait_ge(s_kv, g * (NC + GB))
                    sc.activation(ctxT(HI, k), xaff[:, k % 2, 0:GN], ACT.Copy).then_inc(s_cthi, 1)
                for c in range(NC):
                    act.wait_ge(s_kv, g * (NC + GB) + (c + 1))
                    if c >= 2 or not is_first(g):
                        act.wait_ge(s_kst_out[c % 2], g * 96 + (c // 2) * 48)
                    sc.activation(qT[:, 0, c % 2, HI, 0:GN], KVB[c][:, 0:GN], ACT.Identity, bias=vecs[:, 20 + c:21 + c])\
                      .then_inc(s_khi, 1)

            group(0)
            with act.Fori(1, NG) as g:
                group(g)

            def step(t):
                q = Q_AHEAD
                if t.has(q):
                    t.wait(act, u_qproj, q)
                    t.wait(act, u_smax, q - 4)
                    t.wait_pair(act, s_qst, q - 4, 3 * HG)
                    sc.activation(qT[:, ((t.k + q) // 2) % 2, t.k % 2, HI, :], pA[:, :], ACT.Identity,
                                  bias=vecs[:, 16 + t.chunk(q):17 + t.chunk(q)]).then_inc(u_qhi, 1)
                if t.has(-1):
                    t.wait(act, u_st, -1)
                    t.wait(act, u_av, -2)
                    sc.activation(probs[0:KV, :, :], S[0:KV, :, :], ACT.Exp, scale=SCALE).then_inc(u_exp, 1)
                if t.has(-2):
                    t.wait(act, u_onorm, -2)
                    t.wait(act, u_out, -7)
                    sc.activation(outT[:, HI, (t.k - 2) % (2 * NC), :], onorm[:, t.k % 2, :], ACT.Copy)\
                      .then_inc(u_ohi, 1)
                if t.has(0):
                    t.wait(act, u_mt, 0)
                    t.wait_ring(act, s_mst, -2)
                    sc.activation(mT[:, t.k % 2, :], pA[0:HG, :], ACT.Copy).then_inc(u_mtc, 1)
                    t.wait(act, u_mtc, 0)
                    t.wait(act, u_st, -2)
                    act.dma_start(f(stack[3 * DH:KS, (t.k // 2) % 2, t.k % 2]), f(mT[:, t.k % 2, :]))\
                      .then_inc(s_mst[t.k % 2], 16)
                if t.has(-1):
                    t.wait(act, u_av, -1)
                    t.wait(act, u_onorm, -2)
                    sc.activation(rsum[:, :], pD[:, :], ACT.Ln).then_inc(u_lnsum, 1)
                    t.wait(act, u_lnsum, -1)
                    sc.activation(rsum[:, :], rsum[:, :], ACT.Exp, scale=-1.0).then_inc(u_rsum, 1)
                w = XT_AHEAD
                if t.has(w):
                    par, k = ((t.k + w) // NC) % 2, t.chunk(w)
                    t.wait(act, u_xt, w)
                    t.wait_batch(act, b_aff, w)
                    t.wait_units_of_batch(act, u_qproj, w, back=2)
                    t.wait(act, u_xlo, w - 2)
                    for dst in (xT[:, HI, par, k, :], xaff[:, (t.k + w) % 2, :]):
                        last = sc.activation(dst, pB[:, :], ACT.Identity, bias=affb[:, par, NC + k:NC + k + 1],
                                             scale=affb[:, par, k:k + 1])
                    last.then_inc(u_xaff, 1)

            steps(act, step)

        @block.vector
        def _(dve):
            ve = nc.vector
            ve.memset(minus_half[:, :], -0.5)
            ve.memset(eps4[:, :], EPS)
            ve.memset(one_zero[:, 0:NC], 1.0)
            ve.memset(one_zero[:, NC:2 * NC], 0.0)
            for par in range(2):
                ve.memset(f(kst[3 * DH:KS, par]), 1.0)
            ve.memset(ones[:, :], 1.0).then_inc(s_const, 1)
            dve.wait_ge(s_cexp, 1)
            ve.tensor_scalar(cexp, cexp, 1.0, None, ALU.add).then_inc(s_cden, 1)
            dve.wait_ge(s_cden, 1)
            ve.reciprocal(cexp, cexp).then_inc(s_crec, 1)
            dve.wait_ge(s_crec, 1)
            ve.tensor_tensor(csilu, crow, cexp, ALU.mult).then_inc(s_silu, 1)
            dve.wait_ge(s_early, 1)
            ve.tensor_copy(csT[:, :, :], pA[:, 0:NC * NB].rearrange("p (k b) -> p k b", k=NC))
            ve.tensor_copy(vecs[:, :], pA[:, 256:256 + 24]).then_inc(s_earlyc, 1)
            lo = [outT[:, LO, 0:NC], outT[:, LO, NC:2 * NC], wq[:, LO], wp[:, LO]]
            hi = [outT[:, HI, 0:NC], outT[:, HI, NC:2 * NC], wq[:, HI], wp[:, HI]]

            def split_weight(n):
                dve.wait_ge(s_whi, n + 1)
                ve.tensor_tensor(lo[n], staging[n % 2][:, :, :], f(hi[n]), ALU.subtract).then_inc(s_wlo, 1)

            split_weight(0)
            split_weight(1)
            dve.wait_ge(s_earlyc, 1)
            for n in range(2):
                dve.wait_ge(s_ss, n + 1)
                ve.tensor_tensor(aff[n][:, :, :], (pB, pV)[n][:, 0:2 * NC * NB].rearrange("p (m b) -> p m b", b=NB),
                                 vecs[:, 8 * n:8 * n + 8].rearrange("p (m a) -> p m a", a=1)
                                 .broadcast_to([P, 2 * NC, NB]), ALU.add).then_inc(s_ssb, 1)
            split_weight(2)
            split_weight(3)
            dve.wait_ge(s_bcast, 32)

            def ctx_stats(g):
                dve.wait_ge(s_ctx, g * 16 + 16)
                for b in range(GB):
                    last = ve.bn_stats(bst[0:KV, b, :], cin[:, b, :])
                last.then_inc(s_cst, 1)

            def ctx_aggr():
                for b in range(GB):
                    last = ve.bn_aggr(mv[0:KV, 0, b, :], bst[0:KV, b, :])
                last.then_inc(s_cag, 1)

            def ctx_normalise(g):
                dve.wait_ge(s_crs, g + 1)
                if not is_first(g):
                    dve.wait_ge(s_ct, g * NC)
                for b in range(GB):
                    last = ve.tensor_scalar(hctx[:, b, :], cin[:, b, :], mv[0:KV, 0, b, 0:1], rstd[0:KV, 0, b:b + 1],
                                            ALU.subtract, ALU.mult)
                last.then_inc(s_hctx, 1)

            def ctx_scale(g):
                for k in range(NC):
                    dve.wait_ge(s_ct, g * NC + (k + 1))
                    if k >= 2:
                        dve.wait_ge(s_ctlo, g * NC + (k - 1))
                    scale, bias = (aff[0][:, m, bass.ds(g * GB, GB)].rearrange("p (b a) -> p b a", a=1)
                                   .broadcast_to([P, GB, KV]) for m in (k, NC + k))
                    t3 = xaff[:, k % 2, 0:GN].rearrange("p (b t) -> p b t", b=GB)
                    ve.tensor_tensor(t3, S[:, k, 0:GN].rearrange("p (b t) -> p b t", b=GB), scale, ALU.mult)\
                      .then_inc(s_ctm, 1)
                    dve.wait_ge(s_ctm, g * NC + (k + 1))
                    ve.tensor_tensor(t3, t3, bias, ALU.add).then_inc(s_ctb, 1)

            def k_lo(g):
                for c in range(NC):
                    dve.wait_ge(s_khi, g * NC + (c + 1))
                    ve.scalar_tensor_tensor(out=qT[:, 0, c % 2, LO, 0:GN], in0=KVB[c][:, 0:GN],
                                            scalar=vecs[:, 20 + c:21 + c], in1=f(qT[:, 0, c % 2, HI, 0:GN]),
                                            op0=ALU.add, op1=ALU.subtract).then_inc(s_kvout, 1)

            def v_out(g):
                for b in range(GB):
                    dve.wait_ge(s_kv, g * (NC + GB) + (NC + b + 1))
                    if b >= 2 or not is_first(g):
                        dve.wait_ge(s_v_out[b % 2], g * 32 + (b // 2) * 16)
                    ve.tensor_tensor(onorm[0:KV, b % 2, :], KVB[b][0:KV, :], bv_bc[0:KV, :], ALU.add)\
                      .then_inc(s_kvout, 1)

            ctx_stats(0)
            dve.wait_ge(s_cst, 1)
            ctx_aggr()
            ctx_normalise(0)
            dve.wait_ge(s_aff, 1)

            def group(g):
                ctx_scale(g)
                ctx_stats(g + 1)
                dve.wait_ge(s_cst, g + 2)
                k_lo(g)
                ctx_aggr()
                ctx_normalise(g + 1)
                v_out(g)

            group(0)
            with dve.Fori(1, NG - 1) as g:
                group(g)
            ctx_scale(NG - 1)
            k_lo(NG - 1)
            v_out(NG - 1)

            def step(t):
                if t.has(0):
                    t.wait(dve, u_smax, 0)
                    t.wait(dve, u_mt, -1)
                    ve.tensor_reduce(out=mneg[:, :, :],
                                     in_=S[:, :, 0:HG * KV].rearrange("p t (j n) -> p t j n", j=HG),
                                     axis=AX.X, op=ALU.max, negate=True).then_inc(u_mneg, 1)
                if t.has(-2):
                    t.wait(dve, u_rsum, -2)
                    t.wait(dve, u_olo, -4)
                    ve.tensor_tensor(onorm[:, t.k % 2, :], pV[:, :], rsum[:, :], ALU.mult)
                    ve.tensor_tensor(rsum[:, :], pD[:, :], rsum[:, :], ALU.mult).then_inc(u_rerr, 1)
                    t.wait(dve, u_rerr, -2)
                    ve.scalar_tensor_tensor(out=onorm[:, t.k % 2, :], in0=rsum[:, :], scalar=2.0,
                                            in1=onorm[:, t.k % 2, :], op0=ALU.subtract, op1=ALU.mult,
                                            reverse0=True).then_inc(u_onorm, 1)
                q = Q_AHEAD
                if t.has(q):
                    qu, c = qT[:, ((t.k + q) // 2) % 2, t.k % 2], t.chunk(q)
                    t.wait(dve, u_qhi, q)
                    ve.scalar_tensor_tensor(out=qu[:, LO, :], in0=pA[:, :], scalar=vecs[:, 16 + c:17 + c],
                                            in1=f(qu[:, HI, :]), op0=ALU.add, op1=ALU.subtract).then_inc(u_qlo, 1)
                d = XT_AHEAD
                if t.has(d) and t.chunk(d) == 0:
                    par = ((t.k + d) // NC) % 2
                    t.wait_batch(dve, b_rstd, d)
                    t.wait(dve, u_xt, d - 1)
                    for tt in range(NT):
                        last = ve.tensor_scalar(h[:, tt, :], xin[:, tt, :], mv[:, par, tt, 0:1],
                                                rstd[:, par, tt:tt + 1], ALU.subtract, ALU.mult)
                    last.then_inc(b_h, 1)
                d = XT_AHEAD + 1
                new_batch, par = t.has(d) and t.chunk(d) == 0, ((t.k + d) // NC) % 2
                if new_batch:
                    if t.static:
                        dve.wait_ge(s_x, 16 * ((PAIR * t.i + t.k + d) // NC + 1))
                    else:
                        dve.wait_ge(s_x, t.i * 32 + 16 * ((t.k + d) // NC + 1))
                    for tt in range(NT):
                        last = ve.bn_stats(bst[:, tt, :], xin[:, tt, :])
                    last.then_inc(b_stats, 1)
                    t.wait_batch(dve, b_stats, d)
                    t.wait_units_of_batch(dve, u_xaff, d, back=2)
                    ve.tensor_tensor(affb[:, par, :], one_zero[:, :],
                                     aff[1][:, :, bass.ds(t.batch(d), 1)].rearrange("p c a -> p (c a)"), ALU.add)\
                      .then_inc(b_aff, 1)
                    for tt in range(NT):
                        last = ve.bn_aggr(mv[:, par, tt, :], bst[:, tt, :])
                    last.then_inc(b_aggr, 1)
                if t.has(-OUT_BEHIND):
                    slot = (t.k - OUT_BEHIND) % 4
                    t.wait(dve, u_out, -OUT_BEHIND)
                    t.wait(dve, u_resb, -OUT_BEHIND)
                    ve.tensor_tensor(xres[:, slot, :], pB[:, :], xres[:, slot, :], ALU.add).then_inc(u_y, 1)

            steps(dve, step)

        @block.tensor
        def _(pe):
            te = nc.tensor
            pe.wait_ge(s_ident, 2)
            pe.wait_ge(s_const, 1)
            pe.wait_ge(s_silu, 1)
            for k in range(NC):
                te.transpose(pA[:, k * NB:(k + 1) * NB], csilu[:, k * P:(k + 1) * P], ident[0:NB, 0:NB])
            pe.wait_ge(s_vecrows, 64)
            te.transpose(pA[:, 256:256 + 24], vecrows[:, :], ident[0:24, 0:24]).then_inc(s_early, 1)
            pe.wait_ge(s_earlyc, 1)
            for n in range(2):
                pe.wait_ge(s_wss[n], 16)
                for m in range(2 * NC):
                    for k in range(NC):
                        last = te.matmul((pB, pV)[n][:, m * NB:(m + 1) * NB], wss[n][:, k, m * P:(m + 1) * P],
                                         csT[:, k, :], start=(k == 0), stop=(k == NC - 1))
                last.then_inc(s_ss, 1)
            pe.wait_ge(s_ssb, 2)

            def group(g):
                for k in range(NC):
                    if k == 0:
                        pe.wait_ge(s_hctx, g + 1)
                    if not is_first(g):
                        pe.wait_ge(s_ctm, g * NC + k)
                    for b in range(GB):
                        last = te.transpose(S[:, k, b * KV:(b + 1) * KV], hctx[:, b, k * P:(k + 1) * P],
                                            ident[0:KV, 0:KV])
                    last.then_inc(s_ct, 1)
                pe.wait_ge(s_wlo, 2)
                for c in range(NC):
                    if not is_first(g):
                        pe.wait_ge(s_kvout, g * (NC + GB))
                    n = 0
                    for k in range(NC):
                        if c == 0:
                            pe.wait_ge(s_ctlo, g * NC + (k + 1))
                        for wl, xl in PASSES:
                            last = te.matmul(KVB[c][:, 0:GN], wk(wl, k)[:, c * P:(c + 1) * P], ctxT(xl, k),
                                             start=(n == 0), stop=(n == 3 * NC - 1))
                            n += 1
                    last.then_inc(s_kv, 1)
                for b in range(GB):
                    pe.wait_ge(s_kvout, g * (NC + GB) + (b + 1))
                    n = 0
                    for k in range(NC):
                        for xl, wl in PASSES:
                            last = te.matmul(KVB[b][0:KV, :], ctxT(xl, k)[:, b * KV:(b + 1) * KV], wv(wl, k),
                                             start=(n == 0), stop=(n == 3 * NC - 1))
                            n += 1
                    last.then_inc(s_kv, 1)

            group(0)
            with pe.Fori(1, NG) as g:
                group(g)
            pe.wait_ge(s_wlo, 4)

            def step(t):
                if t.has(0):
                    par = t.k % 2
                    t.wait(pe, u_qhi, 0)
                    t.wait(pe, u_kbd, 0)
                    t.wait(pe, u_exp, -2)
                    for tt in range(NT):
                        last = te.matmul(S[:, tt, 0:HG * KV], qT[:, (t.k // 2) % 2, par, HI, tt * P:(tt + 1) * P],
                                         kbd[:, par].rearrange("p j n -> p (j n)"), start=True, stop=True)
                    last.then_inc(u_smax, 1)
                q = Q_AHEAD
                if t.has(q):
                    c, bpar = t.chunk(q), ((t.k + q) // NC) % 2
                    if c == 0:
                        t.wait_units_of_batch(pe, u_xlo, q)
                    t.wait(pe, u_mtc, -1)
                    if not t.has(-1):
                        t.wait(pe, u_qlo, q - 1)
                    if t.static and t.i == 0 and t.k == -q:
                        pe.wait_ge(s_kvout, NG * (NC + GB))
                    n = 0
                    for k in range(NC):
                        for wl, xl in PASSES:
                            last = te.matmul(pA[:, :], wq[:, wl, k, c * P:(c + 1) * P], xT[:, xl, bpar, k, :],
                                             start=(n == 0), stop=(n == 3 * NC - 1))
                            n += 1
                    last.then_inc(u_qproj, 1)
                if t.has(-1):
                    par = (t.k - 1) % 2
                    t.wait_ring(pe, s_kst, -1)
                    t.wait_pair(pe, s_qst, -1, 3 * HG)
                    t.wait_ring(pe, s_mst, -1)
                    t.wait(pe, u_mneg, 0)
                    for j in range(HG):
                        last = te.matmul(S[0:KV, j, :], kst[0:KS, par, j, :], stack[0:KS, ((t.k - 1) // 2) % 2, par, j, :],
                                         start=True, stop=True)
                    last.then_inc(u_st, 1)
                if t.has(-OUT_BEHIND):
                    tt, half = t.chunk(-OUT_BEHIND), ((t.k - OUT_BEHIND) // NC) % 2 * NC
                    if tt == 0:
                        t.wait_units_of_batch(pe, u_olo, -OUT_BEHIND)
                    t.wait(pe, u_xaff, XT_AHEAD - 1)
                    if not t.has(XT_AHEAD - 1):
                        t.wait(pe, u_y, -OUT_BEHIND - 1)
                    n = 0
                    for k in range(NC):
                        for xl, wl in PASSES:
                            last = te.matmul(pB[:, :], outT[:, xl, half + k, tt * P:(tt + 1) * P], wp[:, wl, k, :],
                                             start=(n == 0), stop=(n == 3 * NC - 1))
                            n += 1
                    last.then_inc(u_out, 1)
                if t.has(0):
                    t.wait(pe, u_mneg, 0)
                    t.wait(pe, u_qlo, Q_AHEAD)
                    if not t.has(Q_AHEAD):
                        t.wait(pe, u_mtc, -1)
                    for tt in range(NT):
                        last = te.transpose(pA[0:HG, tt * P:(tt + 1) * P], f(mneg[:, tt, :]), ident[:, :])
                    last.then_inc(u_mt, 1)
                if t.has(-1):
                    bpar, c = ((t.k - 1) // NC) % 2, t.chunk(-1)
                    t.wait(pe, u_exp, -1)
                    t.wait_batch_dma(pe, s_v, -1)
                    t.wait(pe, u_onorm, -2)
                    for j in range(HG):
                        te.matmul(pV[DH * j:DH * (j + 1), :], vt[0:KV, bpar, (c * HG + j) * DH:(c * HG + j + 1) * DH],
                                  probs[0:KV, j, :], start=True, stop=True)
                    for j in range(HG):
                        last = te.matmul(pD[DH * j:DH * (j + 1), :], ones[0:KV, :], probs[0:KV, j, :],
                                         start=True, stop=True)
                    last.then_inc(u_av, 1)
                w = XT_AHEAD
                if t.has(w):
                    k = t.chunk(w)
                    if k == 0:
                        t.wait_batch(pe, b_h, w)
                    t.wait(pe, u_y, -OUT_BEHIND)
                    t.wait(pe, u_xaff, w - 1)
                    for tt in range(NT):
                        last = te.transpose(pB[:, tt * P:(tt + 1) * P], h[:, tt, k * P:(k + 1) * P], ident[:, :])
                    last.then_inc(u_xt, 1)

            steps(pe, step)


_INS = ["x", "ctx_1024", "cond_1024", "L0_xcond_Wq", "L0_xcond_bq", "L0_xcond_Wkv", "L0_xcond_bkv", "L0_xcond_Wp",
        "L0_xcond_bp", "L0_xcond_Wss_q", "L0_xcond_bss_q", "L0_xcond_Wss_kv", "L0_xcond_bss_kv"]
_OUT = ((16, 512, 512), "float32")


def kernel(**inputs):
    import numpy as _np
    import concourse.bacc as _bacc
    from concourse import mybir as _mybir
    from concourse.bass_utils import run_bass_kernel_spmd as _run

    nc = _bacc.Bacc("TRN2", target_bir_lowering=False, num_devices=1)
    arrays, args = {}, []
    for name in _INS:
        a = _np.ascontiguousarray(inputs[name])
        arrays[f"in_{name}_dram"] = a
        args.append(nc.dram_tensor(f"in_{name}_dram", a.shape, _mybir.dt.from_np(a.dtype), kind="ExternalInput").ap())
    shape, dtype = _OUT
    args.append(nc.dram_tensor("out_0_dram", shape, _mybir.dt.from_np(_np.dtype(dtype)), kind="ExternalOutput").ap())
    adaln_cross_attention_kernel(nc, *args)
    r = _run(nc, [arrays], core_ids=[0])
    return r.results[0]["out_0_dram"]
```

```python
import concourse.bass as bass
from concourse import mybir
from contextlib import ExitStack


def adaln_cross_attention_kernel(
    nc: bass.Bass,
    x: bass.AP,
    ctx_kv: bass.AP,
    cond: bass.AP,
    Wq: bass.AP,
    bq: bass.AP,
    Wkv: bass.AP,
    bkv: bass.AP,
    Wp: bass.AP,
    bp: bass.AP,
    Wss_q: bass.AP,
    bss_q: bass.AP,
    Wss_kv: bass.AP,
    bss_kv: bass.AP,
    out: bass.AP,
):
    f32, f32r = mybir.dt.float32, mybir.dt.float32r
    ALU, ACT, AX = mybir.AluOpType, mybir.ActivationFunctionType, mybir.AxisListType

    P = 128
    NB, L, D = x.shape
    KV = ctx_kv.shape[1]
    NH = 16
    DH = D // NH
    NC = D // P
    NT = L // P
    HG = P // DH
    EPS = 1e-5
    SCALE = float(DH) ** -0.5
    UNITS = NB * NC
    PAIR = 2 * NC
    GB = 4
    NG = NB // GB
    GN = GB * KV
    KS = 3 * DH + 1
    CT = 32
    TN = 2 * D * CT // P
    Q_AHEAD, XT_AHEAD, OUT_BEHIND = 2, 7, 6
    HI, LO = 0, 1
    PASSES = ((HI, HI), (HI, LO), (LO, HI))
    X_AHEAD = XT_AHEAD + 2
    assert NC == NT == HG == 4 and 3 * DH == 96

    x_tiles = x.rearrange("b (t p) n -> (b t) p n", p=P)
    out_tiles = out.rearrange("b (t p) n -> (b t) p n", p=P)
    k_scratch = nc.dram_tensor("k_scratch", [NC, HG, 3 * DH, 1 + NB, KV], f32, kind="Internal").ap()[:, :, :, 1:, :]
    v_scratch = nc.dram_tensor("v_scratch", [NB, KV, D], f32, kind="Internal").ap()

    ctx = ExitStack()
    with ctx:
        def sb(name, shape, dt=f32, where=ctx):
            return where.enter_context(nc.sbuf_tensor(name, shape, dt))

        def sem(name):
            return ctx.enter_context(nc.semaphore(name))

        with ExitStack() as early:
            wss = [sb("wss_kv", [P, NC, 2 * D], f32, early), sb("wss_q", [P, NC, 2 * D], f32, early)]
        xT = sb("xT", [P, 2, 2, NC, L], f32r)
        wq = sb("wq", [P, 2, NC, D], f32r)
        wp = sb("wp", [P, 2, NC, D], f32r)
        outT = sb("outT", [P, 2, 2 * NC, L], f32r)
        stack = sb("stack", [P, 2, 2, HG, L], f32r)
        qT = sb("qT", [P, 2, 2, 2, L], f32r)
        xin = sb("xin", [P, NT, D])
        xres = sb("xres", [P, 4, D])
        h = sb("h", [P, NT, D])
        probs = sb("probs", [P, HG, L])
        onorm = sb("onorm", [P, 2, L])
        rsum = sb("rsum", [P, L])
        xaff = sb("xaff", [P, 2, L])
        kst = sb("kst", [P, 2, HG, KV], f32r)
        kh = sb("kh", [P, 2, KV], f32r)
        kbd = sb("kbd", [P, 2, HG, KV], f32r)
        vt = sb("vt", [P, 2, D])
        bp_bc = sb("bp_bc", [P, D])
        ident = sb("ident", [P, P])
        ones = sb("ones", [P, DH])
        headmask = sb("headmask", [P, HG])
        minus_half = sb("minus_half", [P, 4])
        eps4 = sb("eps4", [P, 4])
        vecrows = sb("vecrows", [24, P])
        vecs = sb("vecs", [P, 24])
        csT = sb("csT", [P, NC, CT])
        aff = [sb("aff_kv", [P, 2 * NC, NB]), sb("aff_q", [P, 2 * NC, NB])]
        one_zero = sb("one_zero", [P, 2 * NC])
        affb = sb("affb", [P, 2, 2 * NC])
        bst = sb("bst", [P, 4, 6])
        mv = sb("mv", [P, 2, 4, 2])
        rstd = sb("rstd", [P, 2, 4])
        mneg = sb("mneg", [P, HG, NT], f32r)
        mT = sb("mT", [HG * NT, 2, P], f32r)

        def wk(hl, k):
            return outT[:, hl, k, :]

        def wv(hl, k):
            return outT[:, hl, NC + k, :]

        def ctxT(g, hl, k):
            return stack[:, g % 2, hl, k, 0:GN]

        def ctx_aff(g, k):
            return (onorm if g == 0 and k >= 2 else xaff)[:, k % 2, 0:GN]

        def kout(c, hl):
            return qT[:, c // 2, c % 2, hl, 0:GN]

        hctx, cin = probs[0:KV], xres[0:KV]
        staging = (xin, h)
        crow, cexp = vt[0:NB, 0, :], vt[0:NB, 1, :]
        csilu, bv_bc = xaff[0:NB, 0, :], rsum

        def f(ap):
            return ap.bitcast(f32)

        table_rows = vt[:, 1, 0:TN]

        S = ctx.enter_context(nc.psum_tensor("S", [P, 4, 512], f32))
        pA = ctx.enter_context(nc.psum_tensor("pA", [P, 512], f32))
        pB = ctx.enter_context(nc.psum_tensor("pB", [P, 512], f32))
        pV = ctx.enter_context(nc.psum_tensor("pV", [P, 512], f32))
        pD = ctx.enter_context(nc.psum_tensor("pD", [P, 512], f32))

        def kv_bank(g, n):
            return (pA, pB, pV, pD)[n % 4] if g < NG - 1 else (pD, pV)[n % 2]

        def kv_wait(eng, g, n):
            n = n - 3 if g < NG - 1 else max(n - 1, 0)
            if g * (NC + GB) + n > 0:
                eng.wait_ge(s_kvout, g * (NC + GB) + n)

        table_bank = (pB[:, 0:TN], S[:, 0, 0:TN])
        tableT_bank = (pV[:, 0:TN], S[:, 3, 0:TN])

        s_wss = [sem("s_wss_kv_in"), sem("s_wss_q_in")]
        s_cond, s_vecrows, s_bv, s_bp = sem("s_cond_in"), sem("s_vecrows_in"), sem("s_bv_in"), sem("s_bp_in")
        s_win = [sem(f"s_weight_in{n}") for n in range(4)]
        s_ctx = sem("s_ctx_in")
        s_const, s_ident, s_mask = sem("s_const"), sem("s_ident"), sem("s_mask")
        s_cexp, s_cden, s_crec, s_silu = sem("s_cexp"), sem("s_cden"), sem("s_crec"), sem("s_silu")
        s_early, s_earlyc = sem("s_early_transposed"), sem("s_early_copied")
        s_ss, s_ssc, s_sst, s_ssb = sem("s_ss"), sem("s_ss_copied"), sem("s_ss_transposed"), sem("s_ss_biased")
        s_whi, s_wlo = sem("s_weight_hi"), sem("s_weight_lo")
        s_cst, s_cag, s_cve, s_crs = sem("s_ctx_stats"), sem("s_ctx_aggr"), sem("s_ctx_vareps"), sem("s_ctx_rstd")
        s_hctx = sem("s_ctx_normalised")
        s_ct, s_ctm, s_ctb, s_cthi, s_ctlo = (sem("s_ctxT"), sem("s_ctxT_scaled"), sem("s_ctxT_biased"),
                                              sem("s_ctxT_hi"), sem("s_ctxT_lo"))
        s_kv, s_kvout, s_khi = sem("s_kv_product"), sem("s_kv_evacuated"), sem("s_k_hi")
        s_kst_out = [sem(f"s_k_stored{c}") for c in range(NC)]
        s_v_out = [sem("s_v_stored0"), sem("s_v_stored1")]
        s_x = sem("s_x_in")
        s_xres = [sem(f"s_xres_in{n}") for n in range(4)]
        s_store = [sem(f"s_y_stored{n}") for n in range(4)]
        s_kst = [sem("s_kst_in0"), sem("s_kst_in1")]
        s_kh = [sem("s_kh_in0"), sem("s_kh_in1")]
        s_v = [sem("s_v_in0"), sem("s_v_in1")]
        s_qst = [sem("s_qstack_in0"), sem("s_qstack_in1")]
        s_mst = [sem("s_mstack_in0"), sem("s_mstack_in1")]
        (u_qproj, u_qhi, u_qlo, u_kbd, u_smax, u_mneg, u_mt, u_mtc, u_st, u_exp, u_av, u_lnsum, u_rsum, u_rerr, u_scaled,
         u_onorm, u_ohi, u_olo, u_out, u_resb, u_y, u_xt, u_xaff, u_xlo) = (sem("u_" + n) for n in (
            "qproj qhi qlo kbd smax mneg mt mtcopied st exp av lnsum rsum rerr scaled onorm outhi outlo out "
            "resbiased y xt xaff xlo").split())
        b_stats, b_aggr, b_vareps, b_rstd, b_h, b_aff = (sem("b_" + n) for n in
                                                         "stats aggr vareps rstd h aff".split())

        block = ctx.enter_context(nc.Block())

        XT0 = -XT_AHEAD


        class Step:

            def __init__(self, i, k):
                self.i, self.k = i, k
                self.static = isinstance(i, int)

            def has(self, d):
                return not self.static or 0 <= PAIR * self.i + self.k + d < UNITS

            def unit(self, d):
                return self.i * PAIR + (self.k + d)

            def batch(self, d):
                return self.i * 2 + (self.k + d) // NC

            def chunk(self, d):
                return (self.k + d) % NC

            def wait(self, eng, s, d, per=1, base=0):
                if not self.static:
                    eng.wait_ge(s, self.i * (PAIR * per) + ((self.k + d + 1) * per + base))
                    return
                n = min(PAIR * self.i + self.k + d + 1, UNITS)
                if n > 0:
                    eng.wait_ge(s, n * per + base)

            def wait_batch(self, eng, s, d, back=0):
                if not self.static:
                    eng.wait_ge(s, self.i * 2 + ((self.k + d) // NC + 1 - back))
                    return
                n = (PAIR * self.i + self.k + d) // NC + 1 - back
                if n > 0:
                    eng.wait_ge(s, n)

            def wait_units_of_batch(self, eng, s, d, back=0):
                if not self.static:
                    eng.wait_ge(s, self.i * PAIR + ((self.k + d) // NC + 1 - back) * NC)
                    return
                n = ((PAIR * self.i + self.k + d) // NC + 1 - back) * NC
                if n > 0:
                    eng.wait_ge(s, n)

            def wait_ring(self, eng, sems, d, dmas=1):
                m = len(sems)
                s = sems[(self.k + d) % m]
                if not self.static:
                    eng.wait_ge(s, self.i * (PAIR // m * 16 * dmas) + ((self.k + d) // m + 1) * 16 * dmas)
                    return
                n = (PAIR * self.i + self.k + d) // m + 1
                if n > 0:
                    eng.wait_ge(s, n * 16 * dmas)

            def wait_pair(self, eng, sems, d, dmas):
                m = (self.k + d) // 2
                n = PAIR // 4 * self.i + m // 2 + 1
                if not self.static or n > 0:
                    eng.wait_ge(sems[m % 2], n * (16 * dmas))

            def wait_batch_dma(self, eng, sems, d):
                bk = (self.k + d) // NC
                if not self.static:
                    eng.wait_ge(sems[bk % 2], self.i * 16 + (bk // 2 + 1) * 16)
                    return
                eng.wait_ge(sems[bk % 2], ((2 * self.i + bk) // 2 + 1) * 16)

        def out_bank(t):
            return pA if t.static and not t.has(0) and t.k % 2 else pB

        def steps(eng, step, first=-X_AHEAD):
            for k in range(first, PAIR - 1):
                step(Step(0, k))
            with eng.Fori(1, NB // 2 - 1) as i:
                for k in range(-1, PAIR - 1):
                    step(Step(i, k))
            for k in range(-1, PAIR + OUT_BEHIND):
                step(Step(NB // 2 - 1, k))

        @block.sync
        def _(sp):
            sp.dma_start(crow, cond).then_inc(s_cond, 16)
            sp.dma_start(cin, ctx_kv[0:GB].rearrange("b t n -> t b n")).then_inc(s_ctx, 16)
            sp.dma_start(wss[0][:, :, :], Wss_kv.rearrange("(k p) n -> p k n", p=P)).then_inc(s_wss[0], 16)
            for row, src in ((0, bss_kv), (8, bss_q), (16, bq), (20, bkv[0:D])):
                n = src.shape[0] // P
                sp.dma_start(vecrows[row:row + n, :], src.rearrange("(a n) -> a n", n=P)).then_inc(s_vecrows, 16)
            weights = [Wkv[:, 0:D], Wkv[:, D:2 * D], Wq, Wp]
            for n in range(2):
                sp.dma_start(staging[n][:, :, :], weights[n].rearrange("(k p) n -> p k n", p=P)).then_inc(s_win[n], 16)
            sp.dma_start(bv_bc[:, :], bkv[D:2 * D].rearrange("(a n) -> a n", a=1).broadcast_to([P, D])).then_inc(s_bv, 16)
            sp.wait_ge(s_hctx, 1)
            sp.dma_start(cin, ctx_kv[GB:2 * GB].rearrange("b t n -> t b n")).then_inc(s_ctx, 16)
            for n in range(2, 4):
                sp.wait_ge(s_whi, n - 1)
                sp.wait_ge(s_wlo, n - 1)
                sp.dma_start(staging[n - 2][:, :, :], weights[n].rearrange("(k p) n -> p k n", p=P)).then_inc(s_win[n], 16)

            def step(t):
                d = X_AHEAD
                if t.chunk(d) == 0 and t.has(d):
                    if t.static and PAIR * t.i + t.k + d == 0:
                        sp.wait_ge(s_whi, 4)
                        sp.wait_ge(s_wlo, 4)
                    t.wait_batch(sp, b_h, d, back=1)
                    sp.dma_start(xin[:, :, :], x[bass.ds(t.batch(d), 1)].rearrange("a (t p) n -> p (a t) n", p=P))\
                      .then_inc(s_x, 16)
                if t.static and PAIR * t.i + t.k == 2:
                    for c in range(NC):
                        sp.wait_ge(s_kst_out[c], 16 * 3 * NG)
                    for par in range(2):
                        sp.wait_ge(s_v_out[par], 16 * NG * GB // 2)
                if t.has(2):
                    t.wait(sp, u_kbd, 0)
                    sp.dma_start(f(kh[:, t.k % 2, :]), k_scratch[t.chunk(2), :, 0:DH, bass.ds(t.batch(2), 1), :])\
                      .then_inc(s_kh[t.k % 2], 16)
                if t.has(1):
                    par = (t.k + 1) % 2
                    t.wait(sp, u_st, -1)
                    sp.dma_start(f(kst[0:3 * DH, par]),
                                 k_scratch[t.chunk(1), :, :, bass.ds(t.batch(1), 1), :]
                                 .rearrange("j r b n -> r j (b n)")).then_inc(s_kst[par], 16)
                q = Q_AHEAD
                if t.has(q) and (t.k + q) % 2:
                    par = ((t.k + q) // 2) % 2
                    t.wait(sp, u_qlo, q)
                    for s, hl in enumerate((HI, HI, LO)):
                        for j in range(HG):
                            sp.dma_start(f(stack[DH * s:DH * (s + 1), par, :, j, :]),
                                         f(qT[DH * j:DH * (j + 1), par, :, hl, :])).then_inc(s_qst[par], 16)
                if t.chunk(1) == 0 and t.has(1):
                    t.wait_units_of_batch(sp, u_av, 1, back=2)
                    par = ((t.k + 1) // NC) % 2
                    sp.dma_start(vt[0:KV, par, :], v_scratch[bass.ds(t.batch(1), 1)].rearrange("a t n -> (a t) n"))\
                      .then_inc(s_v[par], 16)
                if t.has(-OUT_BEHIND):
                    t.wait(sp, u_y, -OUT_BEHIND)
                    slot = (t.k - OUT_BEHIND) % 4
                    sp.dma_start(out_tiles[bass.ds(t.unit(-OUT_BEHIND), 1)].rearrange("a p n -> (a p) n"),
                                 xres[:, slot, :]).then_inc(s_store[slot], 16)
                if t.has(-3):
                    if not (t.static and PAIR * t.i + t.k - 3 < 4):
                        t.wait_ring(sp, s_store, -7)
                    slot = (t.k - 3) % 4
                    sp.dma_start(xres[:, slot, :],
                                 x_tiles[bass.ds(t.unit(-3), 1)].rearrange("a p n -> (a p) n")).then_inc(s_xres[slot], 16)

            for g in range(NG):
                if g == NG - 2:
                    step(Step(0, -X_AHEAD))
                    step(Step(0, XT0 - 1))
                if g == NG - 1:
                    for k in range(XT0, XT0 + 3):
                        step(Step(0, k))
                for c in range(NC):
                    sp.wait_ge(s_kvout, g * (NC + GB) + (c + 1))
                    for s, hl in enumerate((HI, LO, HI)):
                        sp.dma_start(k_scratch[c, :, DH * s:DH * (s + 1), g * GB:(g + 1) * GB, :], f(kout(c, hl)))\
                          .then_inc(s_kst_out[c], 16)
                if g == NG - 1:
                    for k in range(XT0 + 3, -1):
                        step(Step(0, k))
                if g + 2 < NG:
                    sp.wait_ge(s_hctx, g + 2)
                    sp.dma_start(cin, ctx_kv[(g + 2) * GB:(g + 3) * GB].rearrange("b t n -> t b n")).then_inc(s_ctx, 16)
                for b in range(GB):
                    if g == NG - 1 and b == GB - 1:
                        step(Step(0, -1))
                        step(Step(0, 0))
                    sp.wait_ge(s_kvout, g * (NC + GB) + (NC + b + 1))
                    sp.dma_start(v_scratch[g * GB + b], onorm[0:KV, b % 2, :]).then_inc(s_v_out[b % 2], 16)
                if g == 0:
                    sp.dma_start(wss[1][:, :, :], Wss_q.rearrange("(k p) n -> p k n", p=P)).then_inc(s_wss[1], 16)
                    sp.dma_start(bp_bc[:, :], bp.rearrange("(a n) -> a n", a=1).broadcast_to([P, D])).then_inc(s_bp, 16)

            steps(sp, step, 1)
            for s in s_store:
                sp.wait_ge(s, 16 * UNITS // 4)

        @block.gpsimd
        def _(pool):
            gp = nc.gpsimd
            gp.memset(ident[:, :], 0.0).then_inc(s_ident, 1)
            pool.wait_ge(s_ident, 1)
            gp.affine_select(out=ident[:, :], in_=ident[:, :], compare_op=ALU.not_equal, fill=1.0, base=0,
                             pattern=[[-1, P]], channel_multiplier=1).then_inc(s_ident, 1)
            pool.wait_ge(s_ident, 2)
            gp.memset(headmask[:, :], 1.0).then_inc(s_mask, 1)
            pool.wait_ge(s_mask, 1)
            gp.affine_select(out=headmask[:, :], in_=headmask[:, :], compare_op=ALU.is_ge, fill=0.0, base=0,
                             pattern=[[-DH, HG]], channel_multiplier=1).then_inc(s_mask, 1)
            pool.wait_ge(s_mask, 2)
            gp.affine_select(out=headmask[:, :], in_=headmask[:, :], compare_op=ALU.is_ge, fill=0.0, base=DH - 1,
                             pattern=[[DH, HG]], channel_multiplier=-1).then_inc(s_mask, 1)
            pool.wait_ge(s_mask, 3)
            pool.wait_ge(s_const, 1)
            def rstd_of_x(t):
                if t.has(XT_AHEAD + 1) and t.chunk(XT_AHEAD + 1) == 0:
                    par = ((t.k + XT_AHEAD + 1) // NC) % 2
                    t.wait_batch(pool, b_aggr, XT_AHEAD + 1)
                    gp.tensor_tensor(rstd[:, par, :], mv[:, par, :, 1], eps4[:, :], ALU.add).then_inc(b_vareps, 1)
                    t.wait_batch(pool, b_vareps, XT_AHEAD + 1)
                    gp.tensor_tensor(rstd[:, par, :], rstd[:, par, :], minus_half[:, :], ALU.pow).then_inc(b_rstd, 1)

            def step(t):
                if not t.has(0):
                    rstd_of_x(t)
                if t.has(1):
                    par = (t.k + 1) % 2
                    t.wait_ring(pool, s_kh, 1)
                    t.wait(pool, u_smax, -1)
                    gp.tensor_tensor(kbd[:, par],
                                     f(kh[:, par, :]).rearrange("p (a n) -> p a n", a=1).broadcast_to([P, HG, KV]),
                                     headmask[:, :].rearrange("p (j a) -> p j a", a=1).broadcast_to([P, HG, KV]),
                                     ALU.mult).then_inc(u_kbd, 1)
                w = XT_AHEAD - 1
                if t.has(w):
                    par, k = ((t.k + w) // NC) % 2, t.chunk(w)
                    t.wait(pool, u_xaff, w)
                    gp.tensor_tensor(xT[:, LO, par, k, :], xaff[:, (t.k + w) % 2, :], f(xT[:, HI, par, k, :]),
                                     ALU.subtract).then_inc(u_xlo, 1)
                if t.has(-2):
                    t.wait(pool, u_ohi, -2)
                    gp.tensor_tensor(outT[:, LO, (t.k - 2) % (2 * NC), :], onorm[:, t.k % 2, :],
                                     f(outT[:, HI, (t.k - 2) % (2 * NC), :]), ALU.subtract).then_inc(u_olo, 1)
                if t.has(0):
                    rstd_of_x(t)
                if t.has(-5):
                    slot = (t.k - 5) % 4
                    t.wait_ring(pool, s_xres, -5)
                    gp.tensor_tensor(xres[:, slot, :], xres[:, slot, :], bp_bc[:, :], ALU.add).then_inc(u_resb, 1)

            for g in range(NG):
                pool.wait_ge(s_cag, g + 1)
                gp.tensor_tensor(rstd[0:KV, 0, :], mv[0:KV, 0, :, 1], eps4[0:KV, :], ALU.add).then_inc(s_cve, 1)
                pool.wait_ge(s_cve, g + 1)
                gp.tensor_tensor(rstd[0:KV, 0, :], rstd[0:KV, 0, :], minus_half[0:KV, :], ALU.pow).then_inc(s_crs, 1)
                if g == NG - 1:
                    step(Step(0, XT0 - 1))
                for k in range(NC):
                    pool.wait_ge(s_cthi, g * NC + (k + 1))
                    gp.tensor_tensor(ctxT(g, LO, k), ctx_aff(g, k), f(ctxT(g, HI, k)), ALU.subtract)\
                      .then_inc(s_ctlo, 1)
            pool.wait_ge(s_bp, 16)
            steps(pool, step, XT0)

        @block.scalar
        def _(act):
            sc = nc.scalar
            sc.preload_act_table_set("natural_log_exp_and_others")
            act.wait_ge(s_cond, 16)
            sc.activation(cexp, crow, ACT.Exp, scale=-1.0).then_inc(s_cexp, 1)
            weights = [outT[:, HI, 0:NC], outT[:, HI, NC:2 * NC], wq[:, HI], wp[:, HI]]

            def weight_hi(n):
                act.wait_ge(s_win[n], 16)
                sc.activation(weights[n], staging[n % 2][:, :, :], ACT.Copy).then_inc(s_whi, 1)

            def ctx_hi(g):
                for k in range(NC):
                    act.wait_ge(s_ctb, g * NC + (k + 1))
                    if k == 0 and g >= 2:
                        act.wait_ge(s_kv, (g - 1) * (NC + GB))
                    sc.activation(ctxT(g, HI, k), ctx_aff(g, k), ACT.Copy).then_inc(s_cthi, 1)

            def step(t):
                q = Q_AHEAD
                if t.static and PAIR * t.i + t.k + q == 0:
                    for c in range(NC):
                        act.wait_ge(s_kst_out[c], 16 * 3 * NG)
                if t.has(q):
                    t.wait(act, u_qproj, q)
                    t.wait(act, u_smax, q - 4)
                    t.wait_pair(act, s_qst, q - 4, 3 * HG)
                    sc.activation(qT[:, ((t.k + q) // 2) % 2, t.k % 2, HI, :], pA[:, :], ACT.Identity,
                                  bias=vecs[:, 16 + t.chunk(q):17 + t.chunk(q)]).then_inc(u_qhi, 1)
                if t.has(-1):
                    t.wait(act, u_st, -1)
                    t.wait(act, u_av, -2)
                    sc.activation(probs[0:KV, :, :], S[0:KV, :, :], ACT.Exp, scale=SCALE).then_inc(u_exp, 1)
                if t.has(0):
                    t.wait(act, u_mtc, 0)
                    t.wait(act, u_st, -2)
                    act.dma_start(f(stack[3 * DH:KS, (t.k // 2) % 2, t.k % 2]), f(mT[:, t.k % 2, :]))\
                       .then_inc(s_mst[t.k % 2], 16)
                if t.has(-2):
                    t.wait(act, u_onorm, -2)
                    t.wait(act, u_out, -7)
                    sc.activation(outT[:, HI, (t.k - 2) % (2 * NC), :], onorm[:, t.k % 2, :], ACT.Copy)\
                      .then_inc(u_ohi, 1)
                if t.has(-1):
                    t.wait(act, u_av, -1)
                    t.wait(act, u_onorm, -2)
                    sc.activation(rsum[:, :], pD[:, :], ACT.Ln).then_inc(u_lnsum, 1)
                    t.wait(act, u_lnsum, -1)
                    sc.activation(rsum[:, :], rsum[:, :], ACT.Exp, scale=-1.0).then_inc(u_rsum, 1)
                w = XT_AHEAD
                if t.has(w):
                    par, k = ((t.k + w) // NC) % 2, t.chunk(w)
                    t.wait(act, u_xt, w)
                    t.wait_batch(act, b_aff, w)
                    t.wait_units_of_batch(act, u_qproj, w, back=2)
                    t.wait(act, u_xlo, w - 2)
                    for dst in (xT[:, HI, par, k, :], xaff[:, (t.k + w) % 2, :]):
                        last = sc.activation(dst, pB[:, :], ACT.Identity, bias=affb[:, par, NC + k:NC + k + 1],
                                             scale=affb[:, par, k:k + 1])
                    last.then_inc(u_xaff, 1)

            weight_hi(0)
            ctx_hi(0)
            weight_hi(1)
            for g in range(NG):
                for c in range(NC):
                    act.wait_ge(s_kv, g * (NC + GB) + (c + 1))
                    if g > 0:
                        act.wait_ge(s_kst_out[c], g * 48)
                    sc.activation(kout(c, HI), kv_bank(g, c)[:, 0:GN], ACT.Identity, bias=vecs[:, 20 + c:21 + c])\
                      .then_inc(s_khi, 1)
                    if g == NG - 1:
                        step(Step(0, XT0 + c))
                if g + 1 < NG:
                    ctx_hi(g + 1)
                if g == 0:
                    weight_hi(2)
                    weight_hi(3)

            steps(act, step, XT0 + NC)

        @block.vector
        def _(dve):
            ve = nc.vector
            ve.memset(minus_half[:, :], -0.5)
            ve.memset(eps4[:, :], EPS)
            ve.memset(one_zero[:, 0:NC], 1.0)
            ve.memset(one_zero[:, NC:2 * NC], 0.0)
            ve.memset(csT[:, :, :], 0.0)
            for par in range(2):
                ve.memset(f(kst[3 * DH:KS, par]), 1.0)
            ve.memset(ones[:, :], 1.0).then_inc(s_const, 1)
            dve.wait_ge(s_cexp, 1)
            ve.tensor_scalar(cexp, cexp, 1.0, None, ALU.add).then_inc(s_cden, 1)
            dve.wait_ge(s_cden, 1)
            ve.reciprocal(cexp, cexp).then_inc(s_crec, 1)
            dve.wait_ge(s_crec, 1)
            ve.tensor_tensor(csilu, crow, cexp, ALU.mult).then_inc(s_silu, 1)
            dve.wait_ge(s_early, 1)
            ve.tensor_copy(csT[:, :, 0:NB], pA[:, 0:NC * NB].rearrange("p (k b) -> p k b", k=NC))\
              .then_inc(s_earlyc, 1)
            lo = [outT[:, LO, 0:NC], outT[:, LO, NC:2 * NC], wq[:, LO], wp[:, LO]]
            hi = [outT[:, HI, 0:NC], outT[:, HI, NC:2 * NC], wq[:, HI], wp[:, HI]]

            def split_weight(n):
                dve.wait_ge(s_whi, n + 1)
                ve.tensor_tensor(lo[n], staging[n % 2][:, :, :], f(hi[n]), ALU.subtract).then_inc(s_wlo, 1)

            def table_copy(n):
                dve.wait_ge(s_ss, n + 1)
                ve.tensor_copy(table_rows, table_bank[n]).then_inc(s_ssc, 1)

            def table(n):
                dve.wait_ge(s_sst, n + 1)
                for i in range(2):
                    last = ve.tensor_tensor(aff[n][:, i:2 * NC:2, :],
                                            tableT_bank[n][:, i * P:(i + 1) * P].rearrange("p (j b) -> p j b", b=CT)[:, :, 0:NB],
                                            vecs[:, 8 * n + i:8 * n + 8:2].rearrange("p (m a) -> p m a", a=1)
                                            .broadcast_to([P, NC, NB]), ALU.add)
                last.then_inc(s_ssb, 1)

            def ctx_stats(g):
                dve.wait_ge(s_ctx, g * 16 + 16)
                for b in range(GB):
                    last = ve.bn_stats(bst[0:KV, b, :], cin[:, b, :])
                last.then_inc(s_cst, 1)
                dve.wait_ge(s_cst, g + 1)
                for b in range(GB):
                    last = ve.bn_aggr(mv[0:KV, 0, b, :], bst[0:KV, b, :])
                last.then_inc(s_cag, 1)

            def ctx_normalise(g):
                dve.wait_ge(s_crs, g + 1)
                if g > 0:
                    dve.wait_ge(s_ct, g * NC)
                for b in range(GB):
                    last = ve.tensor_scalar(hctx[:, b, :], cin[:, b, :], mv[0:KV, 0, b, 0:1], rstd[0:KV, 0, b:b + 1],
                                            ALU.subtract, ALU.mult)
                last.then_inc(s_hctx, 1)

            def ctx_scale(g, k):
                n = g * NC + k
                dve.wait_ge(s_ct, n + 1)
                if g > 0:
                    dve.wait_ge(s_ctlo, n - 1)
                scale, bias = (aff[0][:, m, g * GB:(g + 1) * GB].rearrange("p (b a) -> p b a", a=1)
                               .broadcast_to([P, GB, KV]) for m in (k, NC + k))
                t3 = ctx_aff(g, k).rearrange("p (b t) -> p b t", b=GB)
                ve.tensor_tensor(t3, S[:, k, 0:GN].rearrange("p (b t) -> p b t", b=GB), scale, ALU.mult)\
                  .then_inc(s_ctm, 1)
                dve.wait_ge(s_ctm, n + 1)
                ve.tensor_tensor(t3, t3, bias, ALU.add).then_inc(s_ctb, 1)

            def k_lo(g, c):
                dve.wait_ge(s_khi, g * NC + (c + 1))
                ve.scalar_tensor_tensor(out=kout(c, LO), in0=kv_bank(g, c)[:, 0:GN], scalar=vecs[:, 20 + c:21 + c],
                                        in1=f(kout(c, HI)), op0=ALU.add, op1=ALU.subtract).then_inc(s_kvout, 1)

            def v_out(g, b):
                dve.wait_ge(s_kv, g * (NC + GB) + (NC + b + 1))
                if g * GB + b >= 2:
                    dve.wait_ge(s_v_out[b % 2], g * 32 + (b // 2) * 16)
                ve.tensor_tensor(onorm[0:KV, b % 2, :], kv_bank(g, NC + b)[0:KV, :], bv_bc[0:KV, :], ALU.add).then_inc(s_kvout, 1)

            def step(t):
                if t.has(0):
                    t.wait(dve, u_smax, 0)
                    t.wait(dve, u_mt, -1)
                    ve.tensor_reduce(out=mneg[:, :, :].rearrange("p j t -> p t j"),
                                     in_=S[:, :, 0:HG * KV].rearrange("p t (j n) -> p t j n", j=HG),
                                     axis=AX.X, op=ALU.max, negate=True).then_inc(u_mneg, 1)
                if t.has(-2):
                    t.wait(dve, u_rsum, -2)
                    t.wait(dve, u_olo, -4)
                    if t.static and PAIR * t.i + t.k == 2:
                        for par in range(2):
                            dve.wait_ge(s_v_out[par], 16 * NG * GB // 2)
                    ve.tensor_tensor(onorm[:, t.k % 2, :], pD[:, :], rsum[:, :], ALU.mult).then_inc(u_rerr, 1)
                    ve.tensor_tensor(rsum[:, :], pV[:, :], rsum[:, :], ALU.mult).then_inc(u_scaled, 1)
                    t.wait(dve, u_scaled, -2)
                    ve.scalar_tensor_tensor(out=onorm[:, t.k % 2, :], in0=onorm[:, t.k % 2, :], scalar=2.0,
                                            in1=rsum[:, :], op0=ALU.subtract, op1=ALU.mult,
                                            reverse0=True).then_inc(u_onorm, 1)
                if t.has(0):
                    t.wait(dve, u_mt, 0)
                    t.wait_ring(dve, s_mst, -2)
                    ve.tensor_copy(mT[:, t.k % 2, :], pD[0:HG * NT, 0:P]).then_inc(u_mtc, 1)
                q = Q_AHEAD
                if t.has(q):
                    qu, c = qT[:, ((t.k + q) // 2) % 2, t.k % 2], t.chunk(q)
                    t.wait(dve, u_qhi, q)
                    ve.scalar_tensor_tensor(out=qu[:, LO, :], in0=pA[:, :], scalar=vecs[:, 16 + c:17 + c],
                                            in1=f(qu[:, HI, :]), op0=ALU.add, op1=ALU.subtract).then_inc(u_qlo, 1)
                d = XT_AHEAD
                to_normalise, par = t.has(d) and t.chunk(d) == 0, ((t.k + d) // NC) % 2

                def normalise(tiles):
                    for tt in tiles:
                        last = ve.tensor_scalar(h[:, tt, :], xin[:, tt, :], mv[:, par, tt, 0:1],
                                                rstd[:, par, tt:tt + 1], ALU.subtract, ALU.mult)
                    return last

                if to_normalise:
                    t.wait_batch(dve, b_rstd, d)
                    t.wait(dve, u_xt, d - 1)
                    normalise(range(NT // 2))
                new, npar = t.has(d + 1) and t.chunk(d + 1) == 0, ((t.k + d + 1) // NC) % 2

                def stats(tiles):
                    for tt in tiles:
                        last = ve.bn_stats(bst[:, tt, :], xin[:, tt, :])
                    return last

                if new:
                    if t.static:
                        dve.wait_ge(s_x, 16 * ((PAIR * t.i + t.k + d + 1) // NC + 1))
                    else:
                        dve.wait_ge(s_x, t.i * 32 + 16 * ((t.k + d + 1) // NC + 1))
                    stats(range(NT // 2))
                if t.has(-OUT_BEHIND):
                    slot = (t.k - OUT_BEHIND) % 4
                    t.wait(dve, u_out, -OUT_BEHIND)
                    t.wait(dve, u_resb, -OUT_BEHIND)
                    ve.tensor_tensor(xres[:, slot, :], out_bank(t)[:, :], xres[:, slot, :], ALU.add).then_inc(u_y, 1)
                if to_normalise:
                    normalise(range(NT // 2, NT)).then_inc(b_h, 1)
                if new:
                    stats(range(NT // 2, NT)).then_inc(b_stats, 1)
                    t.wait_batch(dve, b_stats, d + 1)
                    t.wait_units_of_batch(dve, u_xaff, d + 1, back=2)
                    ve.tensor_tensor(affb[:, npar, :], one_zero[:, :],
                                     aff[1][:, :, bass.ds(t.batch(d + 1), 1)].rearrange("p c a -> p (c a)"), ALU.add)\
                      .then_inc(b_aff, 1)
                    for tt in range(NT):
                        last = ve.bn_aggr(mv[:, npar, tt, :], bst[:, tt, :])
                    last.then_inc(b_aggr, 1)

            ctx_stats(0)
            ctx_normalise(0)
            table_copy(0)
            dve.wait_ge(s_early, 2)
            ve.tensor_scalar(vecs[:, 0:NC], pA[:, 256:256 + NC], 1.0, None, ALU.add)
            ve.tensor_copy(vecs[:, NC:], pA[:, 256 + NC:256 + 24]).then_inc(s_earlyc, 1)
            split_weight(0)
            dve.wait_ge(s_earlyc, 2)
            table(0)
            dve.wait_ge(s_ssb, 1)
            ctx_scale(0, 0)
            ctx_scale(0, 1)
            ctx_scale(0, 2)
            ctx_scale(0, 3)
            ctx_stats(1)
            split_weight(1)
            dve.wait_ge(s_bv, 16)
            for g in range(NG):
                if g + 1 < NG:
                    k_lo(g, 0)
                    k_lo(g, 1)
                    if g == NG - 2:
                        table_copy(1)
                    ctx_normalise(g + 1)
                    k_lo(g, 2)
                    k_lo(g, 3)
                    if g == NG - 2:
                        table(1)
                        step(Step(0, XT0 - 1))
                    ctx_scale(g + 1, 0)
                    for k in range(NC):
                        if k + 1 < NC:
                            ctx_scale(g + 1, k + 1)
                        v_out(g, k)
                        if k == 2 and g + 2 < NG:
                            ctx_stats(g + 2)
                else:
                    for c in range(NC):
                        if c == 0:
                            step(Step(0, XT0))
                        k_lo(g, c)
                        if c == 1:
                            for k in range(XT0 + 1, XT0 + NC):
                                step(Step(0, k))
                    step(Step(0, XT0 + NC))
                    for b in range(GB - 1):
                        v_out(g, b)
                        if b > 0:
                            step(Step(0, XT0 + NC + b))
                    step(Step(0, 0))
                    v_out(g, GB - 1)
                if g < 2:
                    split_weight(2 + g)

            steps(dve, step, XT0 + NC + GB)

        @block.tensor
        def _(pe):
            te = nc.tensor
            pe.wait_ge(s_ident, 2)
            pe.wait_ge(s_const, 1)
            pe.wait_ge(s_silu, 1)
            for k in range(NC):
                last = te.transpose(pA[:, k * NB:(k + 1) * NB], csilu[:, k * P:(k + 1) * P], ident[0:NB, 0:NB])
            last.then_inc(s_early, 1)
            pe.wait_ge(s_earlyc, 1)

            def table(n):
                pe.wait_ge(s_wss[n], 16)
                for k in range(NC):
                    for j in range(P // CT):
                        last = te.matmul(table_bank[n][CT * j:CT * (j + 1), :], csT[:, k, :],
                                         wss[n][:, k, TN * j:TN * (j + 1)], start=(k == 0), stop=(k == NC - 1))
                last.then_inc(s_ss, 1)

            def table_transposed(n):
                pe.wait_ge(s_ssc, n + 1)
                for i in range(TN // P):
                    last = te.transpose(tableT_bank[n][:, i * P:(i + 1) * P], table_rows[:, i * P:(i + 1) * P], ident[:, :])
                last.then_inc(s_sst, 1)

            def ctx_transposed(g):
                pe.wait_ge(s_hctx, g + 1)
                for k in range(NC):
                    if g > 0:
                        pe.wait_ge(s_ctm, (g - 1) * NC + (k + 1))
                    if g == NG - 1 and k == NC - 1:
                        pe.wait_ge(s_ssb, 2)
                    for b in range(GB):
                        last = te.transpose(S[:, k, b * KV:(b + 1) * KV], hctx[:, b, k * P:(k + 1) * P],
                                            ident[0:KV, 0:KV])
                    last.then_inc(s_ct, 1)

            def k_product(g, c):
                if g == 0:
                    pe.wait_ge(s_wlo, 1)
                kv_wait(pe, g, c)
                n = 0
                for k in range(NC):
                    if c == 0:
                        pe.wait_ge(s_ctlo, g * NC + (k + 1))
                    for wl, xl in PASSES:
                        last = te.matmul(kv_bank(g, c)[:, 0:GN], wk(wl, k)[:, c * P:(c + 1) * P], ctxT(g, xl, k),
                                         start=(n == 0), stop=(n == 3 * NC - 1))
                        n += 1
                last.then_inc(s_kv, 1)

            def v_product(g, b):
                if g == 0:
                    pe.wait_ge(s_wlo, 2)
                kv_wait(pe, g, NC + b)
                n = 0
                for k in range(NC):
                    for xl, wl in PASSES:
                        last = te.matmul(kv_bank(g, NC + b)[0:KV, :], ctxT(g, xl, k)[:, b * KV:(b + 1) * KV], wv(wl, k),
                                         start=(n == 0), stop=(n == 3 * NC - 1))
                        n += 1
                last.then_inc(s_kv, 1)

            def scores(t):
                if t.has(-1):
                    par = (t.k - 1) % 2
                    t.wait_ring(pe, s_kst, -1)
                    t.wait_pair(pe, s_qst, -1, 3 * HG)
                    t.wait_ring(pe, s_mst, -1)
                    t.wait(pe, u_mneg, 0)
                    for j in range(HG):
                        last = te.matmul(S[0:KV, j, :], kst[0:KS, par, j, :], stack[0:KS, ((t.k - 1) // 2) % 2, par, j, :],
                                         start=True, stop=True)
                    last.then_inc(u_st, 1)

            def output(t):
                if t.has(-OUT_BEHIND):
                    tt, half = t.chunk(-OUT_BEHIND), ((t.k - OUT_BEHIND) // NC) % 2 * NC
                    t.wait(pe, u_xaff, XT_AHEAD - 1)
                    if not t.has(XT_AHEAD - 1):
                        t.wait(pe, u_y, -OUT_BEHIND - (1 if t.has(-1) else 2))
                    if out_bank(t) is pA:
                        t.wait(pe, u_qlo, Q_AHEAD)
                    n = 0
                    for k in range(NC):
                        if tt == 0:
                            t.wait(pe, u_olo, k - OUT_BEHIND)
                        for xl, wl in PASSES:
                            last = te.matmul(out_bank(t)[:, :], outT[:, xl, half + k, tt * P:(tt + 1) * P], wp[:, wl, k, :],
                                             start=(n == 0), stop=(n == 3 * NC - 1))
                            n += 1
                    last.then_inc(u_out, 1)

            def maxima_transposed(t):
                if t.has(0):
                    t.wait(pe, u_mneg, 0)
                    t.wait(pe, u_rerr, -2)
                    if t.static and PAIR * t.i + t.k == 0:
                        pe.wait_ge(s_kvout, NG * (NC + GB) - 1)
                    te.transpose(pD[0:HG * NT, 0:P], f(mneg[:, :, :]).rearrange("p j t -> p (j t)"), ident[:, :])\
                      .then_inc(u_mt, 1)

            def values(t):
                if t.has(-1):
                    bpar, c = ((t.k - 1) // NC) % 2, t.chunk(-1)
                    t.wait(pe, u_exp, -1)
                    t.wait_batch_dma(pe, s_v, -1)
                    t.wait(pe, u_onorm, -2)
                    t.wait(pe, u_mtc, 0)
                    if t.static and PAIR * t.i + t.k - 1 == 0:
                        pe.wait_ge(s_kvout, NG * (NC + GB))
                    for j in range(HG):
                        te.matmul(pV[DH * j:DH * (j + 1), :], vt[0:KV, bpar, (c * HG + j) * DH:(c * HG + j + 1) * DH],
                                  probs[0:KV, j, :], start=True, stop=True)
                    for j in range(HG):
                        last = te.matmul(pD[DH * j:DH * (j + 1), :], ones[0:KV, :], probs[0:KV, j, :],
                                         start=True, stop=True)
                    last.then_inc(u_av, 1)

            def x_transposed(t):
                w = XT_AHEAD
                if t.has(w):
                    k = t.chunk(w)
                    if k == 0:
                        t.wait_batch(pe, b_h, w)
                    t.wait(pe, u_y, -OUT_BEHIND)
                    t.wait(pe, u_xaff, w - 1)
                    for tt in range(NT):
                        last = te.transpose(pB[:, tt * P:(tt + 1) * P], h[:, tt, k * P:(k + 1) * P], ident[:, :])
                    last.then_inc(u_xt, 1)

            def step(t):
                if t.has(0):
                    par = t.k % 2
                    t.wait(pe, u_qhi, 0)
                    t.wait(pe, u_kbd, 0)
                    t.wait(pe, u_exp, -2)
                    for tt in range(NT):
                        last = te.matmul(S[:, tt, 0:HG * KV], qT[:, (t.k // 2) % 2, par, HI, tt * P:(tt + 1) * P],
                                         kbd[:, par].rearrange("p j n -> p (j n)"), start=True, stop=True)
                    last.then_inc(u_smax, 1)
                q = Q_AHEAD
                if t.has(q):
                    c, bpar = t.chunk(q), ((t.k + q) // NC) % 2
                    t.wait(pe, u_qlo, q - 1)
                    if t.static and PAIR * t.i + t.k + q == 0:
                        pe.wait_ge(s_wlo, 4)
                    n = 0
                    for k in range(NC):
                        if c == 0:
                            t.wait(pe, u_xlo, q + k)
                        for wl, xl in PASSES:
                            last = te.matmul(pA[:, :], wq[:, wl, k, c * P:(c + 1) * P], xT[:, xl, bpar, k, :],
                                             start=(n == 0), stop=(n == 3 * NC - 1))
                            n += 1
                    last.then_inc(u_qproj, 1)
                if t.has(0) and not t.has(Q_AHEAD):
                    output(t)
                    scores(t)
                    maxima_transposed(t)
                else:
                    scores(t)
                    maxima_transposed(t)
                    output(t)
                if t.has(-OUT_BEHIND) or t.chunk(XT_AHEAD) == 0:
                    values(t)
                    x_transposed(t)
                else:
                    x_transposed(t)
                    values(t)

            table(0)
            pe.wait_ge(s_vecrows, 64)
            te.transpose(pA[:, 256:256 + 24], vecrows[:, :], ident[0:24, 0:24]).then_inc(s_early, 1)
            ctx_transposed(0)
            table_transposed(0)
            for g in range(NG):
                for c in range(NC):
                    k_product(g, c)
                    if g == NG - 2 and c == 1:
                        table(1)
                    if g == NG - 1:
                        step(Step(0, XT0 + c))
                if g == NG - 2:
                    table_transposed(1)
                if g + 1 < NG:
                    ctx_transposed(g + 1)
                for b in range(GB):
                    if g == NG - 1 and b == GB - 1:
                        step(Step(0, 0))
                    v_product(g, b)
                    if g == NG - 1 and b < GB - 1:
                        step(Step(0, XT0 + NC + b))

            steps(pe, step, XT0 + NC + GB)


_INS = ["x", "ctx_1024", "cond_1024", "L0_xcond_Wq", "L0_xcond_bq", "L0_xcond_Wkv", "L0_xcond_bkv", "L0_xcond_Wp",
        "L0_xcond_bp", "L0_xcond_Wss_q", "L0_xcond_bss_q", "L0_xcond_Wss_kv", "L0_xcond_bss_kv"]
_OUT = ((16, 512, 512), "float32")


def kernel(**inputs):
    import numpy as _np
    import concourse.bacc as _bacc
    from concourse import mybir as _mybir
    from concourse.bass_utils import run_bass_kernel_spmd as _run

    nc = _bacc.Bacc("TRN2", target_bir_lowering=False, num_devices=1)
    arrays, args = {}, []
    for name in _INS:
        a = _np.ascontiguousarray(inputs[name])
        arrays[f"in_{name}_dram"] = a
        args.append(nc.dram_tensor(f"in_{name}_dram", a.shape, _mybir.dt.from_np(a.dtype), kind="ExternalInput").ap())
    shape, dtype = _OUT
    args.append(nc.dram_tensor("out_0_dram", shape, _mybir.dt.from_np(_np.dtype(dtype)), kind="ExternalOutput").ap())
    adaln_cross_attention_kernel(nc, *args)
    r = _run(nc, [arrays], core_ids=[0])
    return r.results[0]["out_0_dram"]
```
